# Optimizing a Trainium2 kernel written in Bass

```python
import numpy as np
import jax
import jax.numpy as jnp

def _softmax(x, axis=-1):
    return jax.nn.softmax(x, axis=axis)

def _gelu(x):
    return jax.nn.gelu(x, approximate=True)

def _silu(x):
    return jax.nn.silu(x)

def _sigmoid(x):
    return jax.nn.sigmoid(x)

def _layernorm(x, axis=-1, eps=1e-05):
    m = jnp.mean(x, axis=axis, keepdims=True)
    v = jnp.var(x, axis=axis, keepdims=True)
    return (x - m) / jnp.sqrt(v + eps)

def _scatter_add(tgt, idx, src, axis=0):
    return tgt.at[idx].add(src)

def _segment_sum(src, seg, n):
    return jax.ops.segment_sum(src, seg, n)
kernel_name = 'mk_gnn_ffn_d4_gnn_r8_59cba7'

def setup_inputs(seed: int=0):
    np.random.seed(seed)
    _w = jnp.asarray

    def _rec_inputs():
        import jax
        import jax.numpy as jnp
        _gk = jax.random.key(seed)
        x = -6.415e-05 + 1 * jax.random.normal(jax.random.fold_in(_gk, 1), (1250, 512), jnp.float32)
        _s = jax.random.randint(jax.random.fold_in(_gk, 2), (10000,), 0, 1250, jnp.int32)
        _d = jax.random.randint(jax.random.fold_in(_gk, 3), (10000,), 0, 1250, jnp.int32)
        _loop = jnp.arange(1250, dtype=jnp.int32)
        src = jnp.concatenate([_s, _d, _loop])
        dst = jnp.concatenate([_d, _s, _loop])
        _o = jnp.argsort(dst, stable=True)
        src = src[_o]
        dst = dst[_o]
        return (x, src, dst)
    x, src, dst = _rec_inputs()

    def _L0_gnn_setup():
        import jax, jax.numpy as jnp
        import numpy as np
        N_NODES = 2500
        N_EDGES = 18750
        IN_C = 512
        OUT_C = 512
        K_INIT = 7

        def _spmm(row, col, lap, x, num_nodes):
            msgs = lap[:, None] * x[col]
            return jax.ops.segment_sum(msgs, row, num_segments=num_nodes)
        key = jax.random.key(seed)
        k1, k2, k3, k4 = jax.random.split(key, 4)
        x = jax.random.normal(k1, (N_NODES, IN_C), dtype=jnp.float32)
        edge_index = jax.random.randint(k2, (2, N_EDGES), 0, N_NODES, dtype=jnp.int32)
        bound = 1.0 / np.sqrt(IN_C * (K_INIT + 1))
        weight = jax.random.uniform(k3, (K_INIT + 1, IN_C, OUT_C), dtype=jnp.float32, minval=-bound, maxval=bound)
        bias = jax.random.uniform(k4, (OUT_C,), dtype=jnp.float32, minval=-bound, maxval=bound)
        return {'x': x, 'edge_index': edge_index, 'weight': weight, 'bias': bias}
    _L0_gnn_all = _L0_gnn_setup()
    _L0_gnn_in = {k: v for k, v in _L0_gnn_all.items() if k in ('weight', 'bias')}
    del _L0_gnn_all

    def _L0_ffn_setup():
        import jax, jax.numpy as jnp
        import numpy as np
        import math
        B, T, D = (4, 1024, 512)
        E, K, F = (8, 2, 256)
        CAP_FACTOR = 1.25
        key = jax.random.key(seed)
        ks = jax.random.split(key, 4)
        return {'x': jax.random.normal(ks[0], (B, T, D), jnp.float32), 'gate_w': jax.random.normal(ks[1], (E, D), jnp.float32) * 0.01, 'w1': jax.random.normal(ks[2], (E, D, F), jnp.float32) * (1.0 / np.sqrt(D)), 'b1': jnp.zeros((E, F), jnp.float32), 'w2': jax.random.normal(ks[3], (E, F, D), jnp.float32) * (1.0 / np.sqrt(F)), 'b2': jnp.zeros((E, D), jnp.float32)}
    _L0_ffn_all = _L0_ffn_setup()
    _L0_ffn_in = {k: v for k, v in _L0_ffn_all.items() if k in ('gate_w', 'w1', 'b1', 'w2', 'b2')}
    del _L0_ffn_all

    def _L1_gnn_setup():
        import jax, jax.numpy as jnp
        import numpy as np
        N_NODES = 5000
        N_EDGES = 80000
        DIM_H = 512
        N_HEADS = 8
        D_HEAD = DIM_H // N_HEADS

        def _exphormer_attn(x, edge_index, Wq, Wk, Wv):
            N, D = x.shape
            H, d = (N_HEADS, D_HEAD)
            Q = (x @ Wq).reshape(N, H, d)
            K = (x @ Wk).reshape(N, H, d)
            V = (x @ Wv).reshape(N, H, d)
            src, dst = (edge_index[0], edge_index[1])
            scale = np.float32(1.0 / np.sqrt(d))
            score = jnp.einsum('ehd,ehd->eh', K[src], Q[dst]) * scale
            score = jnp.exp(jnp.clip(score, -5.0, 5.0))[..., None]
            msg = V[src] * score
            wV = jax.ops.segment_sum(msg, dst, num_segments=N)
            Z = jax.ops.segment_sum(score, dst, num_segments=N)
            return (wV / (Z + 1e-06)).reshape(N, D)
        key = jax.random.key(seed)
        ks = jax.random.split(key, 8)
        x = jax.random.normal(ks[0], (N_NODES, DIM_H), dtype=jnp.float32)
        edge_index = jax.random.randint(ks[1], (2, N_EDGES), 0, N_NODES, dtype=jnp.int32)
        virt_h = jax.random.normal(ks[2], (1, DIM_H), dtype=jnp.float32)
        virt_edge_index = jnp.zeros((2, 1), dtype=jnp.int32)
        s = 1.0 / np.sqrt(DIM_H)
        Wq = jax.random.normal(ks[3], (DIM_H, DIM_H), dtype=jnp.float32) * s
        Wk = jax.random.normal(ks[4], (DIM_H, DIM_H), dtype=jnp.float32) * s
        Wv = jax.random.normal(ks[5], (DIM_H, DIM_H), dtype=jnp.float32) * s
        bn_gamma = jnp.ones((DIM_H,), dtype=jnp.float32)
        bn_beta = jnp.zeros((DIM_H,), dtype=jnp.float32)
        return {'x': x, 'edge_index': edge_index, 'virt_h': virt_h, 'virt_edge_index': virt_edge_index, 'Wq': Wq, 'Wk': Wk, 'Wv': Wv, 'bn_gamma': bn_gamma, 'bn_beta': bn_beta}
    _L1_gnn_all = _L1_gnn_setup()
    _L1_gnn_in = {k: v for k, v in _L1_gnn_all.items() if k in ('virt_h', 'virt_edge_index', 'Wq', 'Wk', 'Wv', 'bn_gamma', 'bn_beta')}
    del _L1_gnn_all

    def _L1_ffn_setup():
        import jax, jax.numpy as jnp
        import numpy as np
        B, T, D = (4, 1024, 512)
        E, F, CAP = (8, 256, 512)
        key = jax.random.key(seed)
        ks = jax.random.split(key, 6)
        s = 0.02
        return {'x': jax.random.normal(ks[0], (B, T, D), dtype=jnp.float32), 'Wr': jax.random.normal(ks[1], (D, E), dtype=jnp.float32) * s, 'W1': jax.random.normal(ks[2], (E, D, F), dtype=jnp.float32) * s, 'b1': jax.random.normal(ks[3], (E, F), dtype=jnp.float32) * s, 'W2': jax.random.normal(ks[4], (E, F, D), dtype=jnp.float32) * s, 'b2': jax.random.normal(ks[5], (E, D), dtype=jnp.float32) * s}
    _L1_ffn_all = _L1_ffn_setup()
    _L1_ffn_in = {k: v for k, v in _L1_ffn_all.items() if k in ('Wr', 'W1', 'b1', 'W2', 'b2')}
    del _L1_ffn_all

    def _L2_gnn_setup():
        import jax, jax.numpy as jnp
        import numpy as np
        N_NODES = 1250
        N_EDGES = 20000
        IN_DIM = 512
        OUT_DIM = 512
        LN_EPS = 1e-05
        key = jax.random.key(seed)
        k_x, k_src, k_ws, k_wn = jax.random.split(key, 4)
        x = jax.random.normal(k_x, (N_NODES, IN_DIM), dtype=jnp.float32)
        edge_src = jax.random.randint(k_src, (N_EDGES,), 0, N_NODES, dtype=jnp.int32)
        edge_dst = jnp.repeat(jnp.arange(N_NODES, dtype=jnp.int32), N_EDGES // N_NODES)
        deg = jnp.full((N_NODES,), float(N_EDGES // N_NODES), dtype=jnp.float32)
        scale = 1.0 / np.sqrt(IN_DIM)
        W_self = jax.random.normal(k_ws, (OUT_DIM, IN_DIM), dtype=jnp.float32) * scale
        W_neigh = jax.random.normal(k_wn, (OUT_DIM, IN_DIM), dtype=jnp.float32) * scale
        bias = jnp.zeros((OUT_DIM,), dtype=jnp.float32)
        gamma = jnp.ones((OUT_DIM,), dtype=jnp.float32)
        beta = jnp.zeros((OUT_DIM,), dtype=jnp.float32)
        return {'x': x, 'edge_src': edge_src, 'edge_dst': edge_dst, 'deg': deg, 'W_self': W_self, 'W_neigh': W_neigh, 'bias': bias, 'gamma': gamma, 'beta': beta}
    _L2_gnn_all = _L2_gnn_setup()
    _L2_gnn_in = {k: v for k, v in _L2_gnn_all.items() if k in ('W_self', 'W_neigh', 'bias', 'gamma', 'beta')}
    del _L2_gnn_all

    def _L2_ffn_setup():
        import jax, jax.numpy as jnp
        import numpy as np
        B, S, H, E, F = (4, 256, 512, 8, 512)
        key = jax.random.key(seed)
        k = jax.random.split(key, 7)
        x = jax.random.normal(k[0], (B, S, H), dtype=jnp.float32)
        Wr = jax.random.normal(k[1], (H, E), dtype=jnp.float32) / np.sqrt(H)
        br = jnp.zeros((E,), dtype=jnp.float32)
        W1 = jax.random.normal(k[2], (E, H, F), dtype=jnp.float32) / np.sqrt(H)
        b1 = jnp.zeros((E, F), dtype=jnp.float32)
        W2 = jax.random.normal(k[3], (E, F, H), dtype=jnp.float32) / np.sqrt(F)
        b2 = jnp.zeros((E, H), dtype=jnp.float32)
        return {'x': x, 'Wr': Wr, 'br': br, 'W1': W1, 'b1': b1, 'W2': W2, 'b2': b2}
    _L2_ffn_all = _L2_ffn_setup()
    _L2_ffn_in = {k: v for k, v in _L2_ffn_all.items() if k in ('Wr', 'br', 'W1', 'b1', 'W2', 'b2')}
    del _L2_ffn_all

    def _L3_gnn_setup():
        import jax, jax.numpy as jnp
        import numpy as np
        N, E, D = (1250, 20000, 512)

        def _sage_layer(h, src, dst, W_self, W_neigh, b, n_nodes):
            agg = jax.ops.segment_sum(h[src], dst, num_segments=n_nodes)
            deg = jax.ops.segment_sum(jnp.ones_like(dst, dtype=h.dtype), dst, num_segments=n_nodes)
            h_neigh = agg / jnp.maximum(deg, 1.0)[:, None]
            return jax.nn.relu(h @ W_self + h_neigh @ W_neigh + b)
        key = jax.random.key(seed)
        ks = jax.random.split(key, 8)
        scale = 1.0 / np.sqrt(D)
        return {'feats': jax.random.normal(ks[0], (N, D), dtype=jnp.float32), 'src': jax.random.randint(ks[1], (E,), 0, N, dtype=jnp.int32), 'dst': jax.random.randint(ks[2], (E,), 0, N, dtype=jnp.int32), 'W_self1': jax.random.normal(ks[3], (D, D), dtype=jnp.float32) * scale, 'W_neigh1': jax.random.normal(ks[4], (D, D), dtype=jnp.float32) * scale, 'b1': jnp.zeros((D,), dtype=jnp.float32), 'W_self2': jax.random.normal(ks[5], (D, D), dtype=jnp.float32) * scale, 'W_neigh2': jax.random.normal(ks[6], (D, D), dtype=jnp.float32) * scale, 'b2': jnp.zeros((D,), dtype=jnp.float32)}
    _L3_gnn_all = _L3_gnn_setup()
    _L3_gnn_in = {k: v for k, v in _L3_gnn_all.items() if k in ('W_self1', 'W_neigh1', 'b1', 'W_self2', 'W_neigh2', 'b2')}
    del _L3_gnn_all

    def _L3_ffn_setup():
        import jax, jax.numpy as jnp
        import numpy as np
        MAX_THRESHOLD = 0.25
        B, S, D, E = (8, 512, 512, 8)
        key = jax.random.key(seed)
        ks = jax.random.split(key, 5)
        scale = 1.0 / np.sqrt(D)
        return {'inputs': jax.random.normal(ks[0], (B, S, D), dtype=jnp.float32), 'W_gate': jax.random.normal(ks[1], (D, E), dtype=jnp.float32) * scale, 'b_gate': jnp.zeros((E,), dtype=jnp.float32), 'W_thr': jax.random.normal(ks[2], (D, 1), dtype=jnp.float32) * scale, 'b_thr': jnp.zeros((1,), dtype=jnp.float32), 'W_exp': jax.random.normal(ks[3], (E, D, D), dtype=jnp.float32) * scale, 'b_exp': jnp.zeros((E, D), dtype=jnp.float32)}
    _L3_ffn_all = _L3_ffn_setup()
    _L3_ffn_in = {k: v for k, v in _L3_ffn_all.items() if k in ('W_gate', 'b_gate', 'W_thr', 'b_thr', 'W_exp', 'b_exp')}
    del _L3_ffn_all
    return {'x': x, 'src': src, 'dst': dst, 'L0_gnn_weight': _L0_gnn_in['weight'], 'L0_gnn_bias': _L0_gnn_in['bias'], 'L0_ffn_gate_w': _L0_ffn_in['gate_w'], 'L0_ffn_w1': _L0_ffn_in['w1'], 'L0_ffn_b1': _L0_ffn_in['b1'], 'L0_ffn_w2': _L0_ffn_in['w2'], 'L0_ffn_b2': _L0_ffn_in['b2'], 'L1_gnn_virt_h': _L1_gnn_in['virt_h'], 'L1_gnn_virt_edge_index': _L1_gnn_in['virt_edge_index'], 'L1_gnn_Wq': _L1_gnn_in['Wq'], 'L1_gnn_Wk': _L1_gnn_in['Wk'], 'L1_gnn_Wv': _L1_gnn_in['Wv'], 'L1_gnn_bn_gamma': _L1_gnn_in['bn_gamma'], 'L1_gnn_bn_beta': _L1_gnn_in['bn_beta'], 'L1_ffn_Wr': _L1_ffn_in['Wr'], 'L1_ffn_W1': _L1_ffn_in['W1'], 'L1_ffn_b1': _L1_ffn_in['b1'], 'L1_ffn_W2': _L1_ffn_in['W2'], 'L1_ffn_b2': _L1_ffn_in['b2'], 'L2_gnn_W_self': _L2_gnn_in['W_self'], 'L2_gnn_W_neigh': _L2_gnn_in['W_neigh'], 'L2_gnn_bias': _L2_gnn_in['bias'], 'L2_gnn_gamma': _L2_gnn_in['gamma'], 'L2_gnn_beta': _L2_gnn_in['beta'], 'L2_ffn_Wr': _L2_ffn_in['Wr'], 'L2_ffn_br': _L2_ffn_in['br'], 'L2_ffn_W1': _L2_ffn_in['W1'], 'L2_ffn_b1': _L2_ffn_in['b1'], 'L2_ffn_W2': _L2_ffn_in['W2'], 'L2_ffn_b2': _L2_ffn_in['b2'], 'L3_gnn_W_self1': _L3_gnn_in['W_self1'], 'L3_gnn_W_neigh1': _L3_gnn_in['W_neigh1'], 'L3_gnn_b1': _L3_gnn_in['b1'], 'L3_gnn_W_self2': _L3_gnn_in['W_self2'], 'L3_gnn_W_neigh2': _L3_gnn_in['W_neigh2'], 'L3_gnn_b2': _L3_gnn_in['b2'], 'L3_ffn_W_gate': _L3_ffn_in['W_gate'], 'L3_ffn_b_gate': _L3_ffn_in['b_gate'], 'L3_ffn_W_thr': _L3_ffn_in['W_thr'], 'L3_ffn_b_thr': _L3_ffn_in['b_thr'], 'L3_ffn_W_exp': _L3_ffn_in['W_exp'], 'L3_ffn_b_exp': _L3_ffn_in['b_exp']}

def reference(x, src, dst, L0_gnn_weight, L0_gnn_bias, L0_ffn_gate_w, L0_ffn_w1, L0_ffn_b1, L0_ffn_w2, L0_ffn_b2, L1_gnn_virt_h, L1_gnn_virt_edge_index, L1_gnn_Wq, L1_gnn_Wk, L1_gnn_Wv, L1_gnn_bn_gamma, L1_gnn_bn_beta, L1_ffn_Wr, L1_ffn_W1, L1_ffn_b1, L1_ffn_W2, L1_ffn_b2, L2_gnn_W_self, L2_gnn_W_neigh, L2_gnn_bias, L2_gnn_gamma, L2_gnn_beta, L2_ffn_Wr, L2_ffn_br, L2_ffn_W1, L2_ffn_b1, L2_ffn_W2, L2_ffn_b2, L3_gnn_W_self1, L3_gnn_W_neigh1, L3_gnn_b1, L3_gnn_W_self2, L3_gnn_W_neigh2, L3_gnn_b2, L3_ffn_W_gate, L3_ffn_b_gate, L3_ffn_W_thr, L3_ffn_b_thr, L3_ffn_W_exp, L3_ffn_b_exp):
    import jax
    import jax.numpy as jnp

    def _L0_gnn_ref(x, edge_index, weight, bias):
        import jax, jax.numpy as jnp
        import numpy as np
        N_NODES = 2500
        N_EDGES = 18750
        IN_C = 512
        OUT_C = 512
        K_INIT = 7

        def _spmm(row, col, lap, x, num_nodes):
            msgs = lap[:, None] * x[col]
            return jax.ops.segment_sum(msgs, row, num_segments=num_nodes)
        row, col = (edge_index[0], edge_index[1])
        num_nodes = x.shape[0]
        Kw = weight.shape[0]
        deg = jax.ops.segment_sum(jnp.ones_like(row, dtype=x.dtype), row, num_segments=num_nodes)
        dinv = jnp.where(deg > 0, jax.lax.rsqrt(jnp.maximum(deg, 1e-30)), 0.0)
        lap = -dinv[row] * dinv[col]
        Tx_0 = x
        out = Tx_0 @ weight[0]
        Tx_1 = _spmm(row, col, lap, x, num_nodes)
        out = out + Tx_1 @ weight[1]
        for k in range(2, Kw):
            Tx_2 = 2.0 * _spmm(row, col, lap, Tx_1, num_nodes) - Tx_0
            out = out + Tx_2 @ weight[k]
            Tx_0, Tx_1 = (Tx_1, Tx_2)
        return out + bias

    def _L0_ffn_ref(x, gate_w, w1, b1, w2, b2):
        import jax, jax.numpy as jnp
        import numpy as np
        import math
        B, T, D = (4, 1024, 512)
        E, K, F = (8, 2, 256)
        CAP_FACTOR = 1.25
        Bx, Tx, Dx = x.shape
        N = Bx * Tx
        C = math.ceil(CAP_FACTOR * N / E)
        xf = x.reshape(N, Dx)
        probs = jax.nn.softmax(xf @ gate_w.T, axis=-1)
        topk_vals, topk_idx = jax.lax.top_k(probs, K)
        topk_vals = topk_vals / topk_vals.sum(-1, keepdims=True)
        flat_e = topk_idx.reshape(N * K)
        onehot = jax.nn.one_hot(flat_e, E, dtype=jnp.int32)
        pos = jnp.cumsum(onehot, axis=0)[jnp.arange(N * K), flat_e] - 1
        keep = pos < C
        pos_safe = jnp.where(keep, pos, C)
        token_ids = jnp.repeat(jnp.arange(N), K)
        buf = jnp.zeros((E, C + 1, Dx), x.dtype).at[flat_e, pos_safe].set(xf[token_ids])
        expert_in = buf[:, :C]
        h = jax.nn.gelu(jnp.einsum('ecd,edf->ecf', expert_in, w1) + b1[:, None, :], approximate=False)
        expert_out = jnp.einsum('ecf,efd->ecd', h, w2) + b2[:, None, :]
        gathered = expert_out[flat_e, jnp.minimum(pos_safe, C - 1)]
        w = (topk_vals.reshape(N * K) * keep).astype(x.dtype)
        out = (gathered * w[:, None]).reshape(N, K, Dx).sum(axis=1)
        return out.reshape(Bx, Tx, Dx)

    def _L1_gnn_ref(x, edge_index, virt_h, virt_edge_index, Wq, Wk, Wv, bn_gamma, bn_beta):
        import jax, jax.numpy as jnp
        import numpy as np
        N_NODES = 5000
        N_EDGES = 80000
        DIM_H = 512
        N_HEADS = 8
        D_HEAD = DIM_H // N_HEADS

        def _exphormer_attn(x, edge_index, Wq, Wk, Wv):
            N, D = x.shape
            H, d = (N_HEADS, D_HEAD)
            Q = (x @ Wq).reshape(N, H, d)
            K = (x @ Wk).reshape(N, H, d)
            V = (x @ Wv).reshape(N, H, d)
            src, dst = (edge_index[0], edge_index[1])
            scale = np.float32(1.0 / np.sqrt(d))
            score = jnp.einsum('ehd,ehd->eh', K[src], Q[dst]) * scale
            score = jnp.exp(jnp.clip(score, -5.0, 5.0))[..., None]
            msg = V[src] * score
            wV = jax.ops.segment_sum(msg, dst, num_segments=N)
            Z = jax.ops.segment_sum(score, dst, num_segments=N)
            return (wV / (Z + 1e-06)).reshape(N, D)
        h_attn = _exphormer_attn(x, edge_index, Wq, Wk, Wv)
        h = x + h_attn
        mean = jnp.mean(h, axis=0)
        var = jnp.mean(jnp.square(h - mean), axis=0)
        return (h - mean) * jax.lax.rsqrt(var + 1e-05) * bn_gamma + bn_beta

    def _L1_ffn_ref(x, Wr, W1, b1, W2, b2):
        import jax, jax.numpy as jnp
        import numpy as np
        B, T, D = (4, 1024, 512)
        E, F, CAP = (8, 256, 512)
        Bb, Tt, Dd = x.shape
        N = Bb * Tt
        C = min(CAP, N)
        x_flat = x.reshape(N, Dd)
        logits = x_flat @ Wr
        probs = jax.nn.softmax(logits, axis=0)
        vals, idx = jax.lax.top_k(probs.T, C)
        selected = x_flat[idx]
        h = jax.nn.gelu(jnp.einsum('ecd,edf->ecf', selected, W1) + b1[:, None, :], approximate=False)
        out_e = jnp.einsum('ecf,efd->ecd', h, W2) + b2[:, None, :]
        weighted = vals[..., None] * out_e
        output = jnp.zeros_like(x_flat).at[idx.reshape(-1)].add(weighted.reshape(-1, Dd))
        return output.reshape(Bb, Tt, Dd)

    def _L2_gnn_ref(x, edge_src, edge_dst, deg, W_self, W_neigh, bias, gamma, beta):
        import jax, jax.numpy as jnp
        import numpy as np
        N_NODES = 1250
        N_EDGES = 20000
        IN_DIM = 512
        OUT_DIM = 512
        LN_EPS = 1e-05
        n = x.shape[0]
        h_self = jnp.einsum('nd,od->no', x, W_self)
        neigh_sum = jax.ops.segment_sum(x[edge_src], edge_dst, num_segments=n)
        neigh_mean = neigh_sum / jnp.maximum(deg, 1.0)[:, None]
        h_neigh = jnp.einsum('nd,od->no', neigh_mean, W_neigh)
        h = h_self + h_neigh + bias
        mu = jnp.mean(h, axis=-1, keepdims=True)
        var = jnp.mean(jnp.square(h - mu), axis=-1, keepdims=True)
        h = (h - mu) * jax.lax.rsqrt(var + LN_EPS)
        return h * gamma + beta

    def _L2_ffn_ref(x, Wr, br, W1, b1, W2, b2):
        import jax, jax.numpy as jnp
        import numpy as np
        B, S, H, E, F = (4, 256, 512, 8, 512)
        b, s, h = x.shape
        xt = x.reshape(-1, h)
        logits = xt @ Wr + br
        probs = jax.nn.softmax(logits, axis=-1)
        G = jnp.max(probs, axis=-1)
        idx = jnp.argmax(probs, axis=-1)
        h1 = jax.nn.relu(jnp.einsum('nh,ehf->nef', xt, W1) + b1)
        eo = jnp.einsum('nef,efh->neh', h1, W2) + b2
        Eout = jnp.take_along_axis(eo, idx[:, None, None], axis=1)[:, 0, :]
        y = G[:, None] * Eout
        return y.reshape(b, s, h)

    def _L3_gnn_ref(feats, src, dst, W_self1, W_neigh1, b1, W_self2, W_neigh2, b2):
        import jax, jax.numpy as jnp
        import numpy as np
        N, E, D = (1250, 20000, 512)

        def _sage_layer(h, src, dst, W_self, W_neigh, b, n_nodes):
            agg = jax.ops.segment_sum(h[src], dst, num_segments=n_nodes)
            deg = jax.ops.segment_sum(jnp.ones_like(dst, dtype=h.dtype), dst, num_segments=n_nodes)
            h_neigh = agg / jnp.maximum(deg, 1.0)[:, None]
            return jax.nn.relu(h @ W_self + h_neigh @ W_neigh + b)
        n_nodes = feats.shape[0]
        h = _sage_layer(feats, src, dst, W_self1, W_neigh1, b1, n_nodes)
        h = _sage_layer(h, src, dst, W_self2, W_neigh2, b2, n_nodes)
        return h

    def _L3_ffn_ref(inputs, W_gate, b_gate, W_thr, b_thr, W_exp, b_exp):
        import jax, jax.numpy as jnp
        import numpy as np
        MAX_THRESHOLD = 0.25
        B, S, D, E = (8, 512, 512, 8)
        d = inputs.shape[-1]
        x = inputs.reshape(-1, d)
        gate_logits = jax.nn.softmax(x @ W_gate + b_gate, axis=-1)
        thresholds = jax.nn.sigmoid(x @ W_thr + b_thr) * MAX_THRESHOLD
        adapted = gate_logits - thresholds
        selected = (adapted >= 0).astype(x.dtype)
        weights = adapted * selected
        wsum = jnp.sum(weights, axis=-1, keepdims=True)
        wsum = jnp.where(wsum == 0, jnp.ones_like(wsum), wsum)
        weights = weights / wsum
        ex_out = jnp.einsum('td,edf->etf', x, W_exp) + b_exp[:, None, :]
        results = jnp.einsum('etf,te->tf', ex_out, weights)
        return results.reshape(inputs.shape[:-1] + (results.shape[-1],))
    edge_index = jnp.stack([src, dst])
    deg = jnp.maximum(jax.ops.segment_sum(jnp.ones(dst.shape, jnp.float32), dst, num_segments=1250), 1.0)
    x = x + _L0_gnn_ref(_layernorm(x, axis=-1), edge_index, L0_gnn_weight, L0_gnn_bias)
    x = x + _L0_ffn_ref(_layernorm(x, axis=-1)[None], L0_ffn_gate_w, L0_ffn_w1, L0_ffn_b1, L0_ffn_w2, L0_ffn_b2)[0]
    x = x + _L1_gnn_ref(_layernorm(x, axis=-1), edge_index, L1_gnn_virt_h, L1_gnn_virt_edge_index, L1_gnn_Wq, L1_gnn_Wk, L1_gnn_Wv, L1_gnn_bn_gamma, L1_gnn_bn_beta)
    x = x + _L1_ffn_ref(_layernorm(x, axis=-1)[None], L1_ffn_Wr, L1_ffn_W1, L1_ffn_b1, L1_ffn_W2, L1_ffn_b2)[0]
    x = x + _L2_gnn_ref(_layernorm(x, axis=-1), src, dst, deg, L2_gnn_W_self, L2_gnn_W_neigh, L2_gnn_bias, L2_gnn_gamma, L2_gnn_beta)
    x = x + _L2_ffn_ref(_layernorm(x, axis=-1)[None], L2_ffn_Wr, L2_ffn_br, L2_ffn_W1, L2_ffn_b1, L2_ffn_W2, L2_ffn_b2)[0]
    x = x + _L3_gnn_ref(_layernorm(x, axis=-1), src, dst, L3_gnn_W_self1, L3_gnn_W_neigh1, L3_gnn_b1, L3_gnn_W_self2, L3_gnn_W_neigh2, L3_gnn_b2)
    x = x + _L3_ffn_ref(_layernorm(x, axis=-1)[None], L3_ffn_W_gate, L3_ffn_b_gate, L3_ffn_W_thr, L3_ffn_b_thr, L3_ffn_W_exp, L3_ffn_b_exp)[0]
    return x

_drawn_inputs = setup_inputs


def setup_inputs(seed=0):
    import zlib

    import numpy as np

    out = dict(_drawn_inputs(seed))
    spreads = {'L0_ffn_b1': (0.0, 0.1),
     'L0_ffn_b2': (0.0, 0.1),
     'L1_gnn_bn_gamma': (1.0, 0.2),
     'L1_gnn_bn_beta': (0.0, 0.1),
     'L2_gnn_bias': (0.0, 0.1),
     'L2_gnn_gamma': (1.0, 0.2),
     'L2_gnn_beta': (0.0, 0.1),
     'L2_ffn_br': (0.0, 0.1),
     'L2_ffn_b1': (0.0, 0.653),
     'L2_ffn_b2': (0.0, 0.446),
     'L3_gnn_b1': (0.0, 0.311),
     'L3_gnn_b2': (0.0, 0.285),
     'L3_ffn_b_gate': (0.0, 0.1),
     'L3_ffn_b_exp': (0.0, 0.293)}
    factors = {'L1_ffn_Wr': 8.0,
     'L1_ffn_W1': 8.0,
     'L1_ffn_b1': 64.0,
     'L1_ffn_W2': 8.0,
     'L1_ffn_b2': 189.989}
    for name, (base, spread) in spreads.items():
        noise = np.random.default_rng([zlib.crc32(name.encode()), seed]).standard_normal(out[name].shape)
        drawn = base * np.exp(spread * noise) if base else spread * noise
        out[name] = jnp.asarray(drawn.astype(out[name].dtype))
    for name, factor in factors.items():
        out[name] = (out[name] * factor).astype(out[name].dtype)
    return out
```

```python
from collections import namedtuple
from contextlib import ExitStack, contextmanager

import concourse.bass as bass
import numpy as np
from concourse import mybir

P = 128
N = 1250
NT = -(-N // P)
NP = NT * P
D = 512
DC = D // P
NEDGE = 21250
ET = 2 * -(-NEDGE // (2 * P))
EU = ET // 2
E = 8
CHUNKS = [(0, 512), (512, 512), (1024, NP - 1024)]
HEADS, DH = 8, 64
LN_EPS = 1e-5

F32 = mybir.dt.float32
F16 = mybir.dt.float16
BF16 = mybir.dt.bfloat16
I32 = mybir.dt.int32
ALU = mybir.AluOpType
ACT = mybir.ActivationFunctionType
X = mybir.AxisListType.X


class Kept:
    pass


class Chain:

    def __init__(self, eng, sem, base=0):
        self.eng, self.sem, self.base, self.n = eng, sem, base, 0

    def __call__(self, instruction):
        instruction.then_inc(self.sem, 1)
        self.n += 1
        self.eng.wait_ge(self.sem, self.base + self.n)


@contextmanager
def stage(nc, name, *sems):
    handles = [nc.alloc_semaphore(f"{name}_{s}") for s in sems]
    parts = namedtuple("Stage", ["block", "sbuf", "psum", *sems])
    ctx = ExitStack()

    def sbuf(n, shape, dt):
        return ctx.enter_context(nc.sbuf_tensor(f"{name}_{n}", shape, dt))

    def psum(n, shape):
        return ctx.enter_context(nc.psum_tensor(f"{name}_{n}", shape, F32))

    with ctx:
        with nc.Block() as block:
            yield parts(block, sbuf, psum, *handles)
    nc.clear_and_free_semaphores(handles)
    nc.all_engine_barrier()


def tile_of(buf, i):
    return buf[:, bass.ds(i, 1), :].rearrange("p a n -> p (a n)")


def col(buf, i):
    return buf[:, bass.ds(i, 1)]


def constants(nc, g):
    g.ident = g.keep("ident", [P, P], F32)
    g.ident16 = g.keep("ident16", [P, P], F16)
    g.before = g.keep("before", [P, P], F32)
    g.ones = g.keep("ones", [P, P], F32)
    g.zeros16 = g.keep("zeros16", [P, D], F16)
    with stage(nc, "const", "filled", "done") as s:
        @s.block.gpsimd
        def _(pool):
            pool.memset(g.ones[:], 1.0).then_inc(s.filled, 1)
            pool.memset(g.zeros16[:], 0.0).then_inc(s.filled, 1)
            pool.memset(g.ident[:], 0.0).then_inc(s.filled, 1)
            pool.wait_ge(s.filled, 3)
            pool.affine_select(out=g.ident[:], in_=g.ident[:], compare_op=ALU.not_equal, fill=1.0,
                               base=0, pattern=[[-1, P]], channel_multiplier=1).then_inc(s.done, 1)
            pool.affine_select(out=g.before[:], in_=g.ones[:], compare_op=ALU.is_gt, fill=0.0,
                               base=0, pattern=[[1, P]], channel_multiplier=-1).then_inc(s.done, 1)
            pool.wait_ge(s.done, 2)
            pool.tensor_copy(g.ident16[:], g.ident[:]).then_inc(s.done, 1)


def graph(nc, g, a):
    g.by_dst = g.keep("by_dst", [P, NT, NP], F16)
    g.by_src = g.keep("by_src", [P, NT, NP], F16)
    g.deg_dst = g.keep("deg_dst", [P, NT], F32)
    g.deg_src = g.keep("deg_src", [P, NT], F32)
    with stage(nc, "graph", "edges_in", "floats", "ge_ready", "sums_ready", "table_ready", "chain",
               "pool_chain", "hot_ready0", "hot_ready1", "hot_free0", "hot_free1", "rows_ready", "rows_read",
               "turn_ready0", "turn_ready1", "turn_read0", "turn_read1", "rows_kept", "turned", "x_in") as s:
        src_i = s.sbuf("src_i", [P, ET], I32)
        dst_i = s.sbuf("dst_i", [P, ET], I32)
        src = s.sbuf("src", [P, 2 * ET], F32)
        dst = s.sbuf("dst", [P, 2 * ET], F32)
        at_least = s.sbuf("at_least", [P, NT + 1, ET], BF16)
        ones16 = s.sbuf("ones16", [P, 1], BF16)
        nodes_i = s.sbuf("nodes_i", [P, NP], I32)
        nodes = s.sbuf("nodes", [P, NP], F16)
        up_i = s.sbuf("up_i", [1, ET], I32)
        up = s.sbuf("up", [1, ET], F32)
        down = s.sbuf("down", [1, ET], F32)
        found = s.sbuf("found", [1, NT + 1, ET], F32)
        here = s.sbuf("here", [1, ET], F32)
        scored = s.sbuf("scored", [1, ET], F32)
        lim = s.sbuf("lim", [1, 3, NT], F32)
        table = s.sbuf("table", [1, 3, NT], I32)
        hot_dst = s.sbuf("hot_dst", [P, 2, P], F16)
        hot_src = s.sbuf("hot_src", [P, 2, NP], F16)
        rows = s.psum("rows", [P, 3, 512])
        turn = s.psum("turn", [P, 3, 512])
        hot_ready = [s.hot_ready0, s.hot_ready1]
        hot_free = [s.hot_free0, s.hot_free1]
        per_bank = 512 // ET

        @s.block.sync
        def _(sp):
            sp.dma_start(src_i[:], a.src).then_inc(s.edges_in, 16)
            sp.dma_start(dst_i[:], a.dst).then_inc(s.edges_in, 16)
            sp.dma_start(g.x[:], a.x).then_inc(s.x_in, 16)
            sp.wait_ge(s.x_in, 16)

        @s.block.gpsimd
        def _(pool):
            chain = Chain(pool, s.pool_chain)
            chain(pool.memset(ones16[:], 1.0))
            chain(pool.iota(nodes_i[:], [[1, NP]], base=0, channel_multiplier=0))
            chain(pool.iota(up_i[:], [[1, EU], [0, 2]], base=1, channel_multiplier=0))
            pool.tensor_copy(nodes[:], nodes_i[:]).then_inc(s.floats, 1)
            chain(pool.tensor_copy(up[:], up_i[:]))
            pool.tensor_scalar(down[:], up[:], -1.0, float(EU + 1), ALU.mult, ALU.add).then_inc(s.floats, 1)


        @s.block.vector
        def _(dve):
            chain = Chain(dve, s.chain)
            dve.wait_ge(s.edges_in, 32)
            chain(dve.tensor_copy(src[:, 0:ET], src_i[:]))
            chain(dve.tensor_copy(dst[:, 0:ET], dst_i[:]))
            for b in range(NT + 1):
                dve.tensor_scalar(at_least[:, b, :], dst[:, 0:ET], float(b * P), None, ALU.is_ge).then_inc(s.ge_ready, 1)
            dve.wait_ge(s.floats, 2)
            dve.wait_ge(s.sums_ready, 1)
            for b in range(NT + 1):
                part = (rows if b // per_bank < 3 else turn)[0:1, (b // per_bank) % 3,
                                                            (b % per_bank) * ET:(b % per_bank + 1) * ET]
                chain(dve.tensor_copy(found[:, b, :], part))
            for b in range(NT):
                chain(dve.tensor_tensor(here[:], found[:, b, :], found[:, b + 1, :], ALU.is_gt))
                chain(dve.tensor_tensor(scored[:], here[:], up[:], ALU.mult))
                chain(dve.tensor_reduce(lim[:, 1, b:b + 1], scored[:], X, ALU.max))
                chain(dve.tensor_tensor(scored[:], here[:], down[:], ALU.mult))
                chain(dve.tensor_reduce(lim[:, 0, b:b + 1], scored[:], X, ALU.max))
            chain(dve.tensor_scalar(lim[:, 0, :], lim[:, 0, :], 1.0, None, ALU.max))
            chain(dve.tensor_scalar(lim[:, 0, :], lim[:, 0, :], -1.0, float(EU), ALU.mult, ALU.add))
            chain(dve.tensor_tensor(lim[:, 1, :], lim[:, 1, :], lim[:, 0, :], ALU.subtract))
            chain(dve.tensor_scalar(lim[:, 1, :], lim[:, 1, :], 1.0, None, ALU.max))
            chain(dve.memset(lim[:, 2, 0:1], 0.0))
            for b in range(1, NT):
                chain(dve.tensor_tensor(lim[:, 2, b:b + 1], lim[:, 2, b - 1:b], lim[:, 1, b - 1:b], ALU.add))
            chain(dve.tensor_copy(table[:, 0:3, :], lim[:, 0:3, :]))
            dve.sem_inc(s.table_ready, 1)
            with dve.Fori(0, NT) as b:
                first = dve.value_load(table[0:1, 0, bass.ds(b, 1)], min_val=0, max_val=EU - 1)
                visits = dve.value_load(table[0:1, 1, bass.ds(b, 1)], min_val=1, max_val=EU)
                done = dve.value_load(table[0:1, 2, bass.ds(b, 1)], min_val=0, max_val=NT * EU)
                with dve.Fori(0, visits) as u:
                    for h in range(2):
                        dve.wait_ge(hot_free[h], done + u + 1)
                        dve.tensor_scalar(hot_dst[:, h, :], nodes[:, bass.ds(b * P, P)], col(dst, (first + u) * 2 + h),
                                          None, ALU.is_equal)
                        dve.tensor_scalar(hot_src[:, h, :], nodes[:], col(src, (first + u) * 2 + h), None,
                                          ALU.is_equal).then_inc(hot_ready[h], 1)
            dve.wait_ge(s.rows_kept, NT + 1)
            dve.tensor_reduce(g.deg_dst[:], g.by_dst[:], X, ALU.add)
            dve.wait_ge(s.turned, NT)
            dve.tensor_reduce(g.deg_src[:], g.by_src[:], X, ALU.add)

        @s.block.tensor
        def _(pe):
            pe.sem_inc(s.hot_free0, 1)
            pe.sem_inc(s.hot_free1, 1)
            pe.wait_ge(s.ge_ready, NT + 1)
            pe.wait_ge(s.pool_chain, 1)
            for b0 in range(0, NT + 1, per_bank):
                n = min(per_bank, NT + 1 - b0)
                bank = b0 // per_bank
                last = pe.matmul((rows if bank < 3 else turn)[0:1, bank % 3, 0:n * ET], ones16[:, 0:1],
                                 at_least[:, b0:b0 + n, :].rearrange("p b t -> p (b t)"), start=True, stop=True)
            last.then_inc(s.sums_ready, 1)
            pe.wait_ge(s.table_ready, 1)
            with pe.Fori(0, NT) as b:
                pe.wait_ge(s.rows_kept, b + 1)
                for c, (c0, n) in enumerate(CHUNKS):
                    pe.matmul(rows[:, c, 0:n], g.zeros16[:, 0:P], g.zeros16[:, 0:n], start=True, stop=True)
                first = pe.value_load(table[0:1, 0, bass.ds(b, 1)], min_val=0, max_val=EU - 1)
                visits = pe.value_load(table[0:1, 1, bass.ds(b, 1)], min_val=1, max_val=EU)
                done = pe.value_load(table[0:1, 2, bass.ds(b, 1)], min_val=0, max_val=NT * EU)
                with pe.Fori(0, visits) as u:
                    for h in range(2):
                        pe.wait_ge(hot_ready[h], done + u + 1)
                        for c, (c0, n) in enumerate(CHUNKS):
                            last = pe.matmul(rows[:, c, 0:n], hot_dst[:, h, :], hot_src[:, h, c0:c0 + n],
                                             start=False, stop=False, skip_group_check=True)
                        last.then_inc(hot_free[h], 1)
                pe.wait_ge(hot_free[1], done + visits + 1)
                pe.sem_inc(s.rows_ready, 1)
            pe.wait_ge(s.rows_kept, NT + 1)
            with pe.Fori(0, NT // 2) as j:
                for h, bank in enumerate((rows, turn)):
                    if h == 0:
                        pe.wait_ge(s.turn_read0, j + 1)
                    else:
                        pe.wait_ge(s.turn_read1, j + 1)
                    for i in range(NT):
                        last = pe.matmul(bank[:, i // 4, (i % 4) * P:(i % 4 + 1) * P],
                                         g.by_dst[:, i, bass.ds(j * (2 * P) + h * P, P)], g.ident16[:],
                                         start=True, stop=True)
                    last.then_inc(s.turn_ready0 if h == 0 else s.turn_ready1, 1)

        @s.block.scalar
        def _(act):
            for signal in (s.rows_kept, s.turn_read0, s.turn_read1):
                act.sem_inc(signal, 1)
            with act.Fori(0, NT) as b:
                act.wait_ge(s.rows_ready, b + 1)
                for c, (c0, n) in enumerate(CHUNKS):
                    last = act.activation(g.by_dst[:, bass.ds(b, 1), c0:c0 + n].rearrange("p a n -> p (a n)"),
                                          rows[:, c, 0:n], ACT.Copy)
                last.then_inc(s.rows_kept, 1)
            with act.Fori(0, NT // 2) as j:
                for h, bank in enumerate((rows, turn)):
                    act.wait_ge(s.turn_ready0 if h == 0 else s.turn_ready1, j + 1)
                    for c, (c0, n) in enumerate(CHUNKS):
                        last = act.activation(
                            g.by_src[:, bass.ds(j * 2 + h, 1), c0:c0 + n].rearrange("p a n -> p (a n)"),
                            bank[:, c, 0:n], ACT.Copy)
                    last.then_inc(s.turn_read0 if h == 0 else s.turn_read1, 1)
                    act.wait_ge(s.turn_read0 if h == 0 else s.turn_read1, j + 2)
                    act.sem_inc(s.turned, 1)


def layernorm(nc, g, name):
    with stage(nc, f"{name}_ln", "stats", "chain", "var_ready", "root_ready", "rows_ready0", "rows_ready1",
               "rows_free0", "rows_free1", "turn_ready0", "turn_ready1", "turn_free0", "turn_free1") as s:
        stats = s.sbuf("stats", [P, NT, 6], F32)
        mv = s.sbuf("mv", [P, NT, 2], F32)
        var = s.sbuf("var", [P, NT], F32)
        root = s.sbuf("root", [P, NT], F32)
        rstd = s.sbuf("rstd", [P, NT], F32)
        mean = s.sbuf("mean", [P, NT], F32)
        rows = s.sbuf("rows", [P, 2, D], F32)
        turned = [s.psum(f"turned{h}", [P, DC, P]) for h in range(2)]
        rows_ready, rows_free = [s.rows_ready0, s.rows_ready1], [s.rows_free0, s.rows_free1]
        turn_ready, turn_free = [s.turn_ready0, s.turn_ready1], [s.turn_free0, s.turn_free1]

        @s.block.vector
        def _(dve):
            for t in range(NT):
                dve.bn_stats(stats[:, t, :], g.x[:, t, :]).then_inc(s.stats, 1)
            dve.wait_ge(s.stats, NT)
            for t in range(NT):
                dve.bn_aggr(mv[:, t, :], stats[:, t, :]).then_inc(s.stats, 1)
            dve.wait_ge(s.stats, 2 * NT)
            chain = Chain(dve, s.chain)
            chain(dve.tensor_scalar(var[:], mv[:, :, 1], LN_EPS, None, ALU.add))
            dve.sem_inc(s.var_ready, 1)
            chain(dve.tensor_copy(mean[:], mv[:, :, 0]))
            dve.wait_ge(s.root_ready, 1)
            newton_root(dve, chain, rstd[:], var[:], root[:])
            chain(dve.reciprocal(rstd[:], root[:]))
            with dve.Fori(0, NT // 2) as i:
                for h in range(2):
                    dve.wait_ge(rows_free[h], i + 1)
                    dve.tensor_scalar(rows[:, h, :], tile_of(g.x, i * 2 + h), col(mean, i * 2 + h),
                                      col(rstd, i * 2 + h), ALU.subtract, ALU.mult).then_inc(rows_ready[h], 1)


        @s.block.tensor
        def _(pe):
            pe.sem_inc(rows_free[0], 1)
            pe.sem_inc(rows_free[1], 1)
            with pe.Fori(0, NT // 2) as i:
                for h in range(2):
                    pe.wait_ge(rows_ready[h], i + 1)
                    pe.wait_ge(turn_free[h], i + 1)
                    for c in range(DC):
                        last = pe.transpose(turned[h][:, c, :], rows[:, h, c * P:(c + 1) * P], g.ident[:])
                    last.then_inc(turn_ready[h], 1)
                    pe.wait_ge(turn_ready[h], i + 1)
                    pe.sem_inc(rows_free[h], 1)

        @s.block.scalar
        def _(act):
            act.wait_ge(s.var_ready, 1)
            act.activation(root[:], var[:], ACT.Sqrt).then_inc(s.root_ready, 1)
            act.sem_inc(turn_free[0], 1)
            act.sem_inc(turn_free[1], 1)
            with act.Fori(0, NT // 2) as i:
                for h in range(2):
                    act.wait_ge(turn_ready[h], i + 1)
                    act.activation(g.ht[:, :, bass.ds(i * (2 * P) + h * P, P)], turned[h][:],
                                   ACT.Copy).then_inc(turn_free[h], 1)


def newton_root(dve, chain, tmp, square, root):
    chain(dve.reciprocal(tmp, root))
    chain(dve.tensor_tensor(tmp, tmp, square, ALU.mult))
    chain(dve.tensor_tensor(root, root, tmp, ALU.add))
    chain(dve.tensor_scalar(root, root, 0.5, None, ALU.mult))


def cheb(nc, g, a):
    K = a.l0_w.shape[0]
    dinv = g.dinv_src
    with stage(nc, "cheb", "w_in0", "w_in1", "bias_in", "zeroed", "tile_ready", "half_done",
               "b_ready", "hi_ready", "lo_ready", "scaled") as s:
        b_buf = [s.sbuf(f"b{h}", [P, NT, D], F32) for h in range(2)]
        hi = [s.sbuf(f"hi{h}", [P, NT, D], F16) for h in range(2)]
        lo = [s.sbuf(f"lo{h}", [P, NT, D], F16) for h in range(2)]
        w = [s.sbuf(f"w{h}", [P, DC, D], F32) for h in range(2)]
        bias = s.sbuf("bias", [P, D], F32)
        minus2 = s.sbuf("minus2", [P, NT], F32)
        minus1 = s.sbuf("minus1", [P, NT], F32)
        pw = [s.psum(f"pw{i}", [P, D]) for i in range(4)]
        pa = [s.psum(f"pa{i}", [P, D]) for i in range(4)]
        w_in = [s.w_in0, s.w_in1]

        @s.block.sync
        def _(sp):
            sp.dma_start(bias[:], a.l0_bias.partition_broadcast(P)).then_inc(s.bias_in, 16)
            for st in range(2):
                sp.dma_start(w[st][:], a.l0_w[K - 1 - st].rearrange("(c p) n -> p c n", p=P)).then_inc(w_in[st], 16)
            with sp.Fori(1, K // 2) as i:
                for h in range(2):
                    sp.wait_ge(s.tile_ready, i * (2 * NT) + (h - 1) * NT)
                    sp.dma_start(w[h][:], a.l0_w[bass.ds(i * -2 + (K - 1 - h), 1)]
                                 .rearrange("a (c p) n -> p (a c) n", p=P)).then_inc(w_in[h], 16)
            sp.wait_ge(s.bias_in, 16)

        def pe_step(pe, st, h, turn, first=False):
            pe.wait_ge(w_in[h], (turn + 1) * 16)
            for t in range(NT):
                k = t % 4 if h == 0 else (t + 2) % 4
                if not (first and t < 4):
                    pe.wait_ge(s.b_ready, st * NT + (t - 3))
                for c in range(DC):
                    last = pe.matmul(pw[k][:], g.ht[:, c, t * P:(t + 1) * P], w[h][:, c, :],
                                     start=c == 0, stop=c == DC - 1)
                if first:
                    last.then_inc(s.tile_ready, 1)
                    continue
                if t == 0:
                    pe.wait_ge(s.hi_ready, st * NT)
                    pe.wait_ge(s.lo_ready, st * NT)
                for j in range(NT):
                    for part in (hi, lo):
                        last = pe.matmul(pa[k][:], g.by_dst[:, j, t * P:(t + 1) * P], part[1 - h][:, j, :],
                                         start=j == 0 and part is hi, stop=j == NT - 1 and part is lo)
                last.then_inc(s.tile_ready, 1)

        @s.block.tensor
        def _(pe):
            pe_step(pe, 0, 0, 0, first=True)
            with pe.Fori(0, K // 2 - 1) as i:
                pe_step(pe, i * 2 + 1, 1, i)
                pe_step(pe, i * 2 + 2, 0, i + 1)
            pe_step(pe, K - 1, 1, K // 2 - 1)

        def dve_step(dve, st, h, first=False):
            b = b_buf[h]

            def low(t):
                dve.wait_ge(s.hi_ready, st * NT + (t + 1))
                dve.scalar_tensor_tensor(lo[h][:, t, :], b[:, t, :], dinv[:, t:t + 1], hi[h][:, t, :],
                                         ALU.mult, ALU.subtract).then_inc(s.lo_ready, 1)

            for t in range(NT):
                k = t % 4 if h == 0 else (t + 2) % 4
                dve.wait_ge(s.tile_ready, st * NT + (t + 1))
                if first:
                    dve.tensor_copy(b[:, t, :], pw[k][:]).then_inc(s.b_ready, 1)
                else:
                    dve.scalar_tensor_tensor(b[:, t, :], pa[k][:], minus2[:, t:t + 1], b[:, t, :], ALU.mult, ALU.subtract).then_inc(s.half_done, 1)
                    dve.wait_ge(s.half_done, (st - 1) * NT + (t + 1))
                    dve.tensor_tensor(b[:, t, :], b[:, t, :], pw[k][:], ALU.add).then_inc(s.b_ready, 1)
                if t > 0:
                    low(t - 1)
            low(NT - 1)

        def last_step(dve):
            st, b = K - 1, b_buf[1]
            for t in range(NT):
                k = (t + 2) % 4
                n = (K - 2) * NT + 3 * t
                dve.wait_ge(s.tile_ready, st * NT + t + 1)
                dve.scalar_tensor_tensor(b[:, t, :], pa[k][:], minus1[:, t:t + 1], b[:, t, :],
                                         ALU.mult, ALU.subtract).then_inc(s.half_done, 1)
                dve.wait_ge(s.half_done, n + 1)
                dve.tensor_tensor(b[:, t, :], b[:, t, :], bias[:], ALU.add).then_inc(s.half_done, 1)
                dve.wait_ge(s.half_done, n + 2)
                dve.tensor_tensor(b[:, t, :], b[:, t, :], g.x[:, t, :], ALU.add).then_inc(s.half_done, 1)
                dve.wait_ge(s.half_done, n + 3)
                dve.tensor_tensor(g.x[:, t, :], b[:, t, :], pw[k][:], ALU.add).then_inc(s.b_ready, 1)

        @s.block.vector
        def _(dve):
            dve.memset(b_buf[1][:], 0.0).then_inc(s.zeroed, 1)
            dve.tensor_scalar(minus2[:], dinv[:], -2.0, None, ALU.mult).then_inc(s.zeroed, 1)
            dve.tensor_scalar(minus1[:], dinv[:], -1.0, None, ALU.mult).then_inc(s.zeroed, 1)
            dve.wait_ge(s.zeroed, 3)
            dve_step(dve, 0, 0, first=True)
            with dve.Fori(0, K // 2 - 1) as i:
                dve_step(dve, i * 2 + 1, 1)
                dve_step(dve, i * 2 + 2, 0)
            dve.wait_ge(s.bias_in, 16)
            last_step(dve)

        def act_step(act, st, h):
            for t in range(NT):
                act.wait_ge(s.b_ready, st * NT + (t + 1))
                act.activation(hi[h][:, t, :], b_buf[h][:, t, :], ACT.Copy,
                               scale=dinv[:, t:t + 1]).then_inc(s.hi_ready, 1)

        @s.block.scalar
        def _(act):
            act_step(act, 0, 0)
            with act.Fori(0, K // 2 - 1) as i:
                act_step(act, i * 2 + 1, 1)
                act_step(act, i * 2 + 2, 0)


def degrees(nc, g):
    g.dinv_src = g.keep("dinv_src", [P, NT], F32)
    g.rdeg_dst = g.keep("rdeg_dst", [P, NT], F32)
    with stage(nc, "deg", "chain", "root_ready", "square_ready") as s:
        square = s.sbuf("square", [P, NT], F32)
        root = s.sbuf("root", [P, NT], F32)
        tmp = s.sbuf("tmp", [P, NT], F32)
        least = s.sbuf("least", [P, NT], F32)
        some = s.sbuf("some", [P, NT], F32)

        @s.block.scalar
        def _(act):
            act.wait_ge(s.square_ready, 1)
            act.activation(root[:], square[:], ACT.Sqrt).then_inc(s.root_ready, 1)

        @s.block.vector
        def _(dve):
            chain = Chain(dve, s.chain)
            dve.tensor_scalar(square[:], g.deg_src[:], 1.0, None, ALU.max).then_inc(s.square_ready, 1)
            chain(dve.tensor_scalar(some[:], g.deg_src[:], 0.0, None, ALU.is_gt))
            chain(dve.tensor_scalar(least[:], g.deg_dst[:], 1.0, None, ALU.max))
            chain(dve.reciprocal(g.rdeg_dst[:], least[:]))
            dve.wait_ge(s.root_ready, 1)
            newton_root(dve, chain, tmp[:], square[:], root[:])
            chain(dve.reciprocal(tmp[:], root[:]))
            chain(dve.tensor_tensor(g.dinv_src[:], tmp[:], some[:], ALU.mult))


def over_experts(v):
    return v.unsqueeze(2).to_broadcast([P, NT, E])


def over_tiles(v):
    return v.unsqueeze(1).to_broadcast([P, NT, E])


def count_before(dve, chain, mask, acc):
    chain(dve.memset(acc[:, 0, :], 0.0))
    for t in range(1, NT):
        chain(dve.tensor_tensor(acc[:, t, :], acc[:, t - 1, :], mask[:, t - 1, :], ALU.add))


def flat(v):
    return v.rearrange("p t e -> p (t e)")


def route(nc, g, name, w_dram, mode, bias_dram=None, capacity=None):
    M = w_dram.shape[2]
    with stage(nc, f"{name}_route", "w_in", "bias_in", "logits_ready", "shifted", "exp_ready", "chain",
               "mask_ready", "count_ready", "sig_ready", "z_ready") as s:
        w = s.sbuf("w", [P, DC, M], F32)
        bias = s.sbuf("bias", [P, M], F32)
        logits = s.sbuf("logits", [P, NT, E], F32)
        p = s.sbuf("p", [P, NT, E], F32)
        top = s.sbuf("top", [P, NT], F32)
        total = s.sbuf("total", [P, NT], F32)
        rank = s.sbuf("rank", [P, NT, E], F32)
        t1 = s.sbuf("t1", [P, NT, E], F32)
        acc = s.sbuf("acc", [P, NT, E], F32)
        z = s.sbuf("z", [P, NT], F32)
        ez = s.sbuf("ez", [P, NT], F32)
        pl = s.psum("pl", [P, NT, M])
        pc = s.psum("pc", [P, NT * E])

        @s.block.sync
        def _(sp):
            sp.dma_start(w[:], w_dram).then_inc(s.w_in, 16)
            if bias_dram is not None:
                sp.dma_start(bias[:], bias_dram.partition_broadcast(P)).then_inc(s.bias_in, 16)
                sp.wait_ge(s.bias_in, 16)
            sp.wait_ge(s.w_in, 16)

        @s.block.tensor
        def _(pe):
            pe.wait_ge(s.w_in, 16)
            for t in range(NT):
                for c in range(DC):
                    last = pe.matmul(pl[:, t, :], g.ht[:, c, t * P:(t + 1) * P], w[:, c, :],
                                     start=c == 0, stop=c == DC - 1)
            last.then_inc(s.logits_ready, 1)
            if mode == "top2":
                pe.wait_ge(s.mask_ready, 1)
                pe.matmul(pc[:], g.before[:], flat(rank[:]), start=True, stop=False)
                pe.matmul(pc[:], g.ones[:], flat(acc[:]), start=False, stop=True).then_inc(s.count_ready, 1)

        @s.block.scalar
        def _(act):
            act.wait_ge(s.shifted, 1)
            act.activation(p[:], logits[:], ACT.Exp).then_inc(s.exp_ready, 1)
            if mode == "threshold":
                act.wait_ge(s.z_ready, 1)
                act.activation(ez[:], z[:], ACT.Exp, scale=-1.0).then_inc(s.sig_ready, 1)

        @s.block.vector
        def _(dve):
            chain = Chain(dve, s.chain)
            dve.wait_ge(s.logits_ready, 1)
            if bias_dram is not None:
                dve.wait_ge(s.bias_in, 16)
                chain(dve.tensor_tensor(logits[:], pl[:, :, 0:E], over_tiles(bias[:, 0:E]), ALU.add))
            else:
                chain(dve.tensor_copy(logits[:], pl[:, :, 0:E]))
            if mode == "threshold":
                chain(dve.tensor_scalar(z[:], pl[:, :, E], bias[:, E:E + 1], None, ALU.add))
                dve.sem_inc(s.z_ready, 1)
            chain(dve.tensor_reduce(top[:], logits[:], X, ALU.max))
            chain(dve.tensor_tensor(logits[:], logits[:], over_experts(top[:]), ALU.subtract))
            dve.sem_inc(s.shifted, 1)
            dve.wait_ge(s.exp_ready, 1)
            chain(dve.tensor_reduce(total[:], p[:], X, ALU.add))
            chain(dve.reciprocal(total[:], total[:]))
            chain(dve.tensor_tensor(p[:], p[:], over_experts(total[:]), ALU.mult))
            if mode == "threshold":
                dve.wait_ge(s.sig_ready, 1)
                chain(dve.tensor_scalar(ez[:], ez[:], 1.0, None, ALU.add))
                chain(dve.reciprocal(ez[:], ez[:]))
                chain(dve.tensor_scalar(ez[:], ez[:], 0.25, None, ALU.mult))
                chain(dve.tensor_tensor(p[:], p[:], over_experts(ez[:]), ALU.subtract))
                chain(dve.tensor_scalar(p[:], p[:], 0.0, None, ALU.max))
                chain(dve.tensor_reduce(total[:], p[:], X, ALU.add))
                chain(dve.tensor_scalar(top[:], total[:], 0.0, None, ALU.is_equal))
                chain(dve.tensor_tensor(total[:], total[:], top[:], ALU.add))
                chain(dve.reciprocal(total[:], total[:]))
                chain(dve.tensor_tensor(g.gates[:], p[:], over_experts(total[:]), ALU.mult))
                return
            chain(dve.memset(rank[:], 0.0))
            for e in range(E):
                other = p[:, :, e:e + 1]
                if e + 1 < E:
                    chain(dve.tensor_tensor(t1[:, :, e + 1:], p[:, :, e + 1:],
                                            other.to_broadcast([P, NT, E - 1 - e]), ALU.is_le))
                    chain(dve.tensor_tensor(rank[:, :, e + 1:], rank[:, :, e + 1:], t1[:, :, e + 1:], ALU.add))
                if e > 0:
                    chain(dve.tensor_tensor(t1[:, :, :e], p[:, :, :e], other.to_broadcast([P, NT, e]), ALU.is_lt))
                    chain(dve.tensor_tensor(rank[:, :, :e], rank[:, :, :e], t1[:, :, :e], ALU.add))
            chosen = {"top1": 1.0, "top2": 2.0}[mode]
            chain(dve.tensor_scalar(rank[:], rank[:], chosen, None, ALU.is_lt))
            if mode == "top1":
                chain(dve.tensor_tensor(g.gates[:], p[:], rank[:], ALU.mult))
                return
            chain(dve.tensor_tensor(p[:], p[:], rank[:], ALU.mult))
            chain(dve.tensor_reduce(total[:], p[:], X, ALU.add))
            chain(dve.reciprocal(total[:], total[:]))
            chain(dve.tensor_tensor(p[:], p[:], over_experts(total[:]), ALU.mult))
            count_before(dve, chain, rank, acc)
            dve.sem_inc(s.mask_ready, 1)
            dve.wait_ge(s.count_ready, 1)
            chain(dve.tensor_scalar(flat(t1[:]), pc[:], float(capacity), None, ALU.is_lt))
            chain(dve.tensor_tensor(g.gates[:], p[:], t1[:], ALU.mult))


def choose(nc, g, name, w_dram, C):
    BITS = 30
    STEPS = 7
    with stage(nc, f"{name}_choose", "w_in", "logits_ready", "top_ready", "exp_ready", "chain", "p_ready",
               "turned", "mask_ready", "count_ready", "ties_ready", "before_ready", "ones_ready", "loop") as s:
        w = s.sbuf("w", [P, DC, E], F32)
        e_rows = s.sbuf("e_rows", [E, NP], F32)
        top = s.sbuf("top", [E, 1], F32)
        total = s.sbuf("total", [E, 1], F32)
        p = s.sbuf("p", [P, NT, E], F32)
        ones16 = s.sbuf("ones16", [P, P], BF16)
        above = s.sbuf("above", [P, NT, E], BF16)
        limit = s.sbuf("limit", [P, E], I32)
        tried = s.sbuf("tried", [P, E], I32)
        bit = s.sbuf("bit", [P, E], I32)
        passed = s.sbuf("passed", [P, E], I32)
        count = s.sbuf("count", [P, E], F32)
        ties = s.sbuf("ties", [P, NT, E], F32)
        acc = s.sbuf("acc", [P, NT, E], F32)
        more = s.sbuf("more", [P, NT, E], F32)
        pl = s.psum("pl", [P, 3, 512])
        pt = s.psum("pt", [P, NT, E])
        pc = s.psum("pc", [P, NT, E])
        pb = s.psum("pb", [P, NT * E])

        @s.block.sync
        def _(sp):
            sp.dma_start(w[:], w_dram).then_inc(s.w_in, 16)
            sp.wait_ge(s.w_in, 16)

        @s.block.tensor
        def _(pe):
            pe.wait_ge(s.w_in, 16)
            for k, (c0, n) in enumerate(CHUNKS):
                for c in range(DC):
                    last = pe.matmul(pl[0:E, k, 0:n], w[:, c, :], g.ht[:, c, c0:c0 + n],
                                     start=c == 0, stop=c == DC - 1)
            last.then_inc(s.logits_ready, 1)
            pe.wait_ge(s.p_ready, 1)
            for t in range(NT):
                last = pe.transpose(pt[:, t, :], e_rows[:, t * P:(t + 1) * P], g.ident[0:E, 0:E])
            last.then_inc(s.turned, 1)
            with pe.Fori(0, BITS + 1) as i:
                pe.wait_ge(s.mask_ready, i + 1)
                pe.matmul(flat(pc[:]), ones16[:], flat(above[:]), start=True, stop=True).then_inc(s.count_ready, 1)
            pe.wait_ge(s.ties_ready, 1)
            pe.matmul(pb[:], g.before[:], flat(ties[:]), start=True, stop=False)
            pe.matmul(pb[:], g.ones[:], flat(acc[:]), start=False, stop=True).then_inc(s.before_ready, 1)

        @s.block.scalar
        def _(act):
            act.wait_ge(s.top_ready, 1)
            act.activation(e_rows[:, 0:N], pl[0:E].rearrange("p a b -> p (a b)")[:, 0:N], ACT.Exp, bias=top[:],
                           accum_out=total[:]).then_inc(s.exp_ready, 1)

        @s.block.vector
        def _(dve):
            chain = Chain(dve, s.chain)
            chain(dve.memset(ones16[:], 1.0))
            chain(dve.memset(limit[:], 0))
            chain(dve.memset(bit[:], 1 << (BITS - 1)))
            chain(dve.memset(e_rows[:, N:NP], 0.0))
            dve.wait_ge(s.logits_ready, 1)
            chain(dve.tensor_reduce(top[:], pl[0:E].rearrange("p a b -> p (a b)")[:, 0:N], X, ALU.max))
            chain(dve.tensor_scalar(top[:], top[:], -1.0, None, ALU.mult))
            dve.sem_inc(s.top_ready, 1)
            dve.wait_ge(s.exp_ready, 1)
            chain(dve.reciprocal(total[:], total[:]))
            chain(dve.tensor_scalar(e_rows[:], e_rows[:], total[:, 0:1], None, ALU.mult))
            dve.sem_inc(s.p_ready, 1)
            dve.wait_ge(s.turned, 1)
            chain(dve.tensor_copy(p[:], pt[:]))
            with dve.Fori(0, BITS) as i:
                step = Chain(dve, s.loop, i * STEPS)
                step(dve.tensor_tensor(tried[:], limit[:], bit[:], ALU.bitwise_or))
                step(dve.tensor_tensor(above[:], p[:], over_tiles(tried[:].bitcast(F32)), ALU.is_ge))
                dve.sem_inc(s.mask_ready, 1)
                dve.wait_ge(s.count_ready, i + 1)
                step(dve.tensor_reduce(count[:], pc[:].rearrange("p t e -> p e t"), X, ALU.add))
                step(dve.tensor_scalar(passed[:], count[:], float(C), None, ALU.is_ge))
                step(dve.tensor_tensor(passed[:], passed[:], bit[:], ALU.mult))
                step(dve.tensor_tensor(limit[:], limit[:], passed[:], ALU.bitwise_or))
                step(dve.tensor_scalar(bit[:], bit[:], 1, None, ALU.logical_shift_right))
                assert step.n == STEPS
            value = over_tiles(limit[:].bitcast(F32))
            chain(dve.tensor_tensor(above[:], p[:], value, ALU.is_gt))
            dve.sem_inc(s.mask_ready, 1)
            chain(dve.tensor_tensor(ties[:], p[:], value, ALU.is_equal))
            count_before(dve, chain, ties, acc)
            dve.sem_inc(s.ties_ready, 1)
            dve.wait_ge(s.count_ready, BITS + 1)
            chain(dve.tensor_reduce(count[:], pc[:].rearrange("p t e -> p e t"), X, ALU.add))
            chain(dve.tensor_scalar(count[:], count[:], -1.0, float(C), ALU.mult, ALU.add))
            dve.wait_ge(s.before_ready, 1)
            chain(dve.tensor_tensor(more[:], pb[:].rearrange("p (t e) -> p t e", e=E), over_tiles(count[:]),
                                    ALU.is_lt))
            chain(dve.tensor_tensor(ties[:], ties[:], more[:], ALU.mult))
            chain(dve.tensor_tensor(ties[:], ties[:], above[:], ALU.add))
            chain(dve.tensor_tensor(g.gates[:], p[:], ties[:], ALU.mult))


def expert_bias(nc, g, name, b_dram):
    with stage(nc, f"{name}_bias", "b_in", "turned", "gates_ready", "tile_ready", "tile_read") as s:
        b = s.sbuf("b", [E, D], F32)
        gates_t = s.sbuf("gates_t", [E, NP], F32)
        pt = s.psum("pt", [E, 3, 512])
        py = [s.psum(f"py{i}", [P, D]) for i in range(4)]

        @s.block.sync
        def _(sp):
            sp.dma_start(b[:], b_dram).then_inc(s.b_in, 16)
            sp.wait_ge(s.b_in, 16)

        @s.block.tensor
        def _(pe):
            for t in range(NT):
                last = pe.transpose(pt[:, t // 4, (t % 4) * P:(t % 4 + 1) * P], g.gates[:, t, :], g.ident[:])
            last.then_inc(s.turned, 1)
            pe.wait_ge(s.gates_ready, 1)
            pe.wait_ge(s.b_in, 16)
            for t in range(NT):
                if t >= 4:
                    pe.wait_ge(s.tile_read, t - 3)
                pe.matmul(py[t % 4][:], gates_t[:, t * P:(t + 1) * P], b[:], start=True,
                          stop=True).then_inc(s.tile_ready, 1)

        @s.block.vector
        def _(dve):
            dve.wait_ge(s.turned, 1)
            dve.tensor_copy(gates_t[:], pt[:].rearrange("p a b -> p (a b)")[:, 0:NP]).then_inc(s.gates_ready, 1)
            for t in range(NT):
                dve.wait_ge(s.tile_ready, t + 1)
                dve.tensor_tensor(g.x[:, t, :], g.x[:, t, :], py[t % 4][:], ALU.add).then_inc(s.tile_read, 1)


def experts(nc, g, name, F, func, w1_dram, b1_dram, w2_dram):
    FC = F // P
    HG = len(CHUNKS) * FC
    HB, YB = 2 * HG, 2 * NT
    assert HB % 4 == 0 and YB % 4 == 0
    with stage(nc, f"{name}_experts", "w_in0", "w_in1", "h_ready", "h_kept", "y_ready", "y_added") as s:
        w1 = [s.sbuf(f"w1_{h}", [P, DC, F], F32) for h in range(2)]
        b1 = [s.sbuf(f"b1_{h}", [P, FC], F32) for h in range(2)]
        w2 = [s.sbuf(f"w2_{h}", [P, FC, D], F32) for h in range(2)]
        ht = [s.sbuf(f"ht{k}", [P, FC, n], F32) for k, (_, n) in enumerate(CHUNKS)]
        ph = [s.psum(f"ph{i}", [P, 512]) for i in range(4)]
        py = [s.psum(f"py{i}", [P, D]) for i in range(4)]
        w_in = [s.w_in0, s.w_in1]

        @s.block.sync
        def _(sp):
            with sp.Fori(0, E // 2) as i:
                for h in range(2):
                    sp.wait_ge(s.y_ready, i * YB + (h + 1) * NT)
                    e = bass.ds(i * 2 + h, 1)
                    sp.dma_start(w1[h][:], w1_dram[e].rearrange("a (c p) n -> p (a c) n", p=P)).then_inc(w_in[h], 16)
                    sp.dma_start(b1[h][:], b1_dram[e].rearrange("a p n -> p (a n)")).then_inc(w_in[h], 16)
                    sp.dma_start(w2[h][:], w2_dram[e].rearrange("a (c p) n -> p (a c) n", p=P)).then_inc(w_in[h], 16)


        @s.block.tensor
        def _(pe):
            def half(i, h):
                pe.wait_ge(w_in[h], i * 48 + 48)
                order = [("h", 0), ("h", 1), ("y", 0), ("h", 2), ("y", 1), ("y", 2)]
                for kind, k in order:
                    c0, n = CHUNKS[k]
                    if kind == "h":
                        for f in range(FC):
                            u = h * HG + k * FC + f
                            pe.wait_ge(s.h_kept, i * HB + u + 1)
                            for c in range(DC):
                                last = pe.matmul(ph[u % 4][:, 0:n], w1[h][:, c, f * P:(f + 1) * P],
                                                 g.ht[:, c, c0:c0 + n], start=c == 0, stop=c == DC - 1)
                            last.then_inc(s.h_ready, 1)
                    else:
                        pe.wait_ge(s.h_kept, i * HB + h * HG + (k + 1) * FC + 4)
                        for t in range(c0 // P, (c0 + n) // P):
                            v = h * NT + t
                            pe.wait_ge(s.y_added, i * YB + v + 1)
                            for f in range(FC):
                                last = pe.matmul(py[v % 4][:], ht[k][:, f, t * P - c0:(t + 1) * P - c0],
                                                 w2[h][:, f, :], start=f == 0, stop=f == FC - 1)
                            last.then_inc(s.y_ready, 1)

            pe.sem_inc(s.y_ready, 2 * NT)
            with pe.Fori(0, E // 2) as i:
                half(i, 0)
                half(i, 1)

        @s.block.scalar
        def _(act):
            act.sem_inc(s.h_kept, 4)
            with act.Fori(0, E // 2) as i:
                for h in range(2):
                    act.wait_ge(w_in[h], i * 48 + 48)
                    for k, (c0, n) in enumerate(CHUNKS):
                        act.wait_ge(s.y_ready, i * YB + (h + 1) * NT + (c0 + n) // P)
                        for f in range(FC):
                            u = h * HG + k * FC + f
                            act.wait_ge(s.h_ready, i * HB + u + 1)
                            act.activation(ht[k][:, f, :], ph[u % 4][:, 0:n], func,
                                           bias=b1[h][:, f:f + 1]).then_inc(s.h_kept, 1)

        @s.block.vector
        def _(dve):
            dve.sem_inc(s.y_added, 4)
            with dve.Fori(0, E // 2) as i:
                for h in range(2):
                    for t in range(NT):
                        v = h * NT + t
                        dve.wait_ge(s.y_ready, i * YB + v + 1 + 2 * NT)
                        gate = g.gates[:, t, bass.ds(i * 2 + h, 1)]
                        dve.scalar_tensor_tensor(g.x[:, t, :], py[v % 4][:], gate, g.x[:, t, :],
                                                 ALU.mult, ALU.add).then_inc(s.y_added, 1)


def attention(nc, g, a):
    LAG = 3
    PAIRS = HEADS // 2
    EXP_LOW, EXP_HIGH = float(np.exp(np.float32(-5.0))), float(np.exp(np.float32(5.0)))
    NC = len(CHUNKS)
    UNITS = 2 * NC * NT
    OUTS = 2 * NC
    with stage(nc, "attn", "w_in", "w_used", "ones_set", "qk_ready", "qk_kept", "v_ready", "v_kept", "s_ready",
               "exp_ready", "clipped", "p_ready", "p_used", "z_chain", "o_kept") as s:
        wq = s.sbuf("wq", [P, DC, P], F32)
        wk = s.sbuf("wk", [P, DC, P], F32)
        wv = s.sbuf("wv", [P, DC, P], F32)
        qt = s.sbuf("qt", [P, NP], F32)
        kt = s.sbuf("kt", [P, NP], F32)
        v1 = s.sbuf("v1", [P, NT, 2, P], F32)
        e = [s.sbuf(f"e{i}", [P, 512], F32) for i in range(3)]
        pr = [s.sbuf(f"p{i}", [P, 512], F32) for i in range(3)]
        rz = s.sbuf("rz", [DH, 512], F32)
        ps = [s.psum(f"ps{i}", [P, 512]) for i in range(4)]
        po = [s.psum(f"po{i}", [P, 512]) for i in range(2)]
        pq = [s.psum(f"pq{i}", [P, 512]) for i in range(2)]
        units = [(h, k, j) for h in range(2) for k in range(NC) for j in range(NT)]
        v_rounds = [range(0, 4), range(4, 8), range(8, NT)]


        @s.block.sync
        def _(sp):
            with sp.Fori(0, PAIRS) as i:
                sp.wait_ge(s.w_used, i + 1)
                for w, dram in ((wq, a.wq), (wk, a.wk), (wv, a.wv)):
                    sp.dma_start(w[:], dram.rearrange("(c p) n -> p c n", p=P)[:, :, bass.ds(i * P, P)])\
                      .then_inc(s.w_in, 16)

        @s.block.tensor
        def _(pe):
            for signal in (s.w_used, s.s_ready, s.p_used):
                pe.sem_inc(signal, 1)
            with pe.Fori(0, PAIRS) as i:
                pe.wait_ge(s.w_in, i * 48 + 48)
                for m, (w, k) in enumerate([(w, k) for w in (wq, wk) for k in range(NC)]):
                    c0, n = CHUNKS[k]
                    if m >= 2:
                        pe.wait_ge(s.qk_kept, i * (2 * NC) + m - 1)
                    else:
                        pe.wait_ge(s.v_kept, i * 3 + 1)
                    for c in range(DC):
                        last = pe.matmul(pq[m % 2][:, 0:n], w[:, c, :], g.ht[:, c, c0:c0 + n],
                                         start=c == 0, stop=c == DC - 1)
                    last.then_inc(s.qk_ready, 1)
                for r, tiles in enumerate(v_rounds):
                    pe.wait_ge(s.qk_kept, i * (2 * NC) + min(2 * NC, 5 + r))
                    if r == 2:
                        pe.wait_ge(s.v_kept, i * 3 + 2)
                    for t in tiles:
                        for c in range(DC):
                            last = pe.matmul(pq[r % 2][:, (t % 4) * P:(t % 4 + 1) * P],
                                             g.ht[:, c, t * P:(t + 1) * P], wv[:, c, :],
                                             start=c == 0, stop=c == DC - 1)
                    last.then_inc(s.v_ready, 1)
                for u in range(UNITS + LAG):
                    if u < UNITS:
                        h, k, j = units[u]
                        c0, n = CHUNKS[k]
                        if u == 0:
                            pe.wait_ge(s.qk_kept, (i + 1) * (2 * NC))
                        pe.wait_ge(s.exp_ready, i * UNITS + max(u - 3, 0) + 1)
                        rows = slice(h * DH, (h + 1) * DH)
                        pe.matmul(ps[u % 4][:, 0:n], kt[rows, j * P:(j + 1) * P], qt[rows, c0:c0 + n],
                                  start=True, stop=True).then_inc(s.s_ready, 1)
                    if u >= LAG:
                        v = u - LAG
                        h, k, j = units[v]
                        c0, n = CHUNKS[k]
                        o = h * NC + k
                        if v == 0:
                            pe.wait_ge(s.v_kept, (i + 1) * 3 + 1)
                        if j == 0:
                            pe.wait_ge(s.o_kept, i * OUTS + max(o - 1, 0) + 1)
                        pe.wait_ge(s.p_ready, i * UNITS + v + 2)
                        pe.matmul(po[o % 2][:, 0:n], v1[:, j, h, :], pr[v % 3][:, 0:n],
                                  start=j == 0, stop=j == NT - 1).then_inc(s.p_used, 1)
                pe.sem_inc(s.w_used, 1)

        @s.block.scalar
        def _(act):
            act.sem_inc(s.exp_ready, 1)
            with act.Fori(0, PAIRS) as i:
                act.wait_ge(s.s_ready, i * UNITS + 1)
                for m, (t, k) in enumerate([(t, k) for t in (qt, kt) for k in range(NC)]):
                    c0, n = CHUNKS[k]
                    act.wait_ge(s.qk_ready, i * (2 * NC) + m + 1)
                    act.activation(t[:, c0:c0 + n], pq[m % 2][:, 0:n], ACT.Copy).then_inc(s.qk_kept, 1)
                for u, (h, k, j) in enumerate(units):
                    n = CHUNKS[k][1]
                    act.wait_ge(s.s_ready, i * UNITS + u + 2)
                    act.wait_ge(s.p_ready, i * UNITS + max(u - 2, 0) + 1)
                    act.activation(e[u % 3][:, 0:n], ps[u % 4][:, 0:n], ACT.Exp,
                                   scale=DH ** -0.5).then_inc(s.exp_ready, 1)

        @s.block.vector
        def _(dve):
            dve.memset(v1[:], 1.0).then_inc(s.ones_set, 1)
            dve.wait_ge(s.ones_set, 1)
            for signal in (s.v_kept, s.o_kept, s.p_ready):
                dve.sem_inc(signal, 1)
            with dve.Fori(0, PAIRS) as i:
                dve.wait_ge(s.p_used, i * UNITS + 1)
                for r, tiles in enumerate(v_rounds):
                    dve.wait_ge(s.v_ready, i * 3 + r + 1)
                    m = len(tiles)
                    for h in range(2):
                        last = dve.tensor_copy(
                            v1[:, tiles[0]:tiles[0] + m, h, 0:DH],
                            pq[r % 2][:, 0:m * P].rearrange("p (t q) -> p t q", q=P)[:, :, h * DH:(h + 1) * DH])
                    last.then_inc(s.v_kept, 1)

                def keep(o):
                    h, k = divmod(o, NC)
                    c0, n = CHUNKS[k]
                    dve.wait_ge(s.p_used, i * UNITS + (o + 1) * NT + 1)
                    dve.tensor_scalar(rz[:, 0:n], po[o % 2][DH:P, 0:n], 1e-6, None, ALU.add).then_inc(s.z_chain, 1)
                    dve.wait_ge(s.z_chain, i * (2 * OUTS) + 2 * o + 1)
                    dve.reciprocal(rz[:, 0:n], rz[:, 0:n]).then_inc(s.z_chain, 1)
                    dve.wait_ge(s.z_chain, i * (2 * OUTS) + 2 * o + 2)
                    dve.tensor_tensor(g.attn[h * DH:(h + 1) * DH, bass.ds(i, 1), c0:c0 + n]
                                      .rearrange("p a n -> p (a n)"), po[o % 2][0:DH, 0:n], rz[:, 0:n],
                                      ALU.mult).then_inc(s.o_kept, 1)

                for u, (h, k, j) in enumerate(units):
                    c0, n = CHUNKS[k]
                    dve.wait_ge(s.exp_ready, i * UNITS + u + 2)
                    dve.tensor_scalar(e[u % 3][:, 0:n], e[u % 3][:, 0:n], EXP_LOW, EXP_HIGH, ALU.max,
                                      ALU.min).then_inc(s.clipped, 1)
                    dve.wait_ge(s.clipped, i * UNITS + u + 1)
                    dve.wait_ge(s.p_used, i * UNITS + max(u - 2, 0) + 1)
                    dve.tensor_tensor(pr[u % 3][:, 0:n], e[u % 3][:, 0:n], g.by_src[:, j, c0:c0 + n],
                                      ALU.mult).then_inc(s.p_ready, 1)
                    if j == 4 and (h, k) != (0, 0):
                        keep(h * NC + k - 1)
                keep(OUTS - 1)


def batchnorm(nc, g, a):
    PARTS = [(0, 512), (512, 512), (1024, N - 1024)]
    with stage(nc, "bn", "params_in", "summed", "stats", "chain", "var_ready", "root_ready", "tile_ready",
               "tile_read") as s:
        gamma = s.sbuf("gamma", [P, DC], F32)
        beta = s.sbuf("beta", [P, DC], F32)
        stats = s.sbuf("stats", [P, DC, len(PARTS), 6], F32)
        mv = s.sbuf("mv", [P, DC, 2], F32)
        var = s.sbuf("var", [P, DC], F32)
        root = s.sbuf("root", [P, DC], F32)
        tmp = s.sbuf("tmp", [P, DC], F32)
        scale = s.sbuf("scale", [P, DC], F32)
        pt = [s.psum(f"pt{i}", [P, DC, P]) for i in range(4)]

        @s.block.sync
        def _(sp):
            sp.dma_start(gamma[:], a.bn_gamma).then_inc(s.params_in, 16)
            sp.dma_start(beta[:], a.bn_beta).then_inc(s.params_in, 16)
            sp.wait_ge(s.params_in, 32)

        @s.block.scalar
        def _(act):
            act.wait_ge(s.var_ready, 1)
            act.activation(root[:], var[:], ACT.Sqrt).then_inc(s.root_ready, 1)

        @s.block.tensor
        def _(pe):
            pe.wait_ge(s.summed, 2 * DC)
            for t in range(NT):
                if t >= 4:
                    pe.wait_ge(s.tile_read, t - 3)
                for c in range(DC):
                    last = pe.transpose(pt[t % 4][:, c, :], g.attn[:, c, t * P:(t + 1) * P], g.ident[:])
                last.then_inc(s.tile_ready, 1)

        @s.block.vector
        def _(dve):
            for c in range(DC):
                dve.tensor_tensor(g.attn[:, c, :], g.attn[:, c, :], g.ht[:, c, :], ALU.add).then_inc(s.summed, 1)
            dve.wait_ge(s.summed, DC)
            for c in range(DC):
                for k, (c0, n) in enumerate(PARTS):
                    dve.bn_stats(stats[:, c, k, :], g.attn[:, c, c0:c0 + n]).then_inc(s.stats, 1)
            dve.wait_ge(s.stats, DC * len(PARTS))
            for c in range(DC):
                dve.bn_aggr(mv[:, c, :], stats[:, c, :, :].rearrange("p a b -> p (a b)")).then_inc(s.stats, 1)
            dve.wait_ge(s.stats, DC * len(PARTS) + DC)
            chain = Chain(dve, s.chain)
            chain(dve.tensor_scalar(var[:], mv[:, :, 1], 1e-5, None, ALU.add))
            dve.sem_inc(s.var_ready, 1)
            dve.wait_ge(s.root_ready, 1)
            newton_root(dve, chain, tmp[:], var[:], root[:])
            chain(dve.reciprocal(scale[:], root[:]))
            dve.wait_ge(s.params_in, 32)
            chain(dve.tensor_tensor(scale[:], scale[:], gamma[:], ALU.mult))
            chain(dve.tensor_tensor(tmp[:], mv[:, :, 0], scale[:], ALU.mult))
            chain(dve.tensor_tensor(beta[:], beta[:], tmp[:], ALU.subtract))
            for c in range(DC):
                dve.tensor_scalar(g.attn[:, c, :], g.attn[:, c, :], scale[:, c:c + 1], beta[:, c:c + 1],
                                  ALU.mult, ALU.add).then_inc(s.summed, 1)
            for t in range(NT):
                dve.wait_ge(s.tile_ready, t + 1)
                dve.tensor_tensor(g.x[:, t, :], g.x[:, t, :], pt[t % 4][:].rearrange("p c n -> p (c n)"),
                                  ALU.add).then_inc(s.tile_read, 1)


def sage(nc, g, name, w_self_dram, w_neigh_dram, bias_dram, relu, add_to_x):
    with stage(nc, name, "w_in", "bias_in", "y_ready", "hi_ready", "lo_ready", "tile_ready", "tile_read",
               "chain") as s:
        wn = s.sbuf("wn", [P, DC, D], F32)
        ws = s.sbuf("ws", [P, DC, D], F32)
        bias = s.sbuf("bias", [P, D], F32)
        hi = s.sbuf("hi", [P, NT, D], F16)
        lo = s.sbuf("lo", [P, NT, D], F16)
        tmp = [s.sbuf(f"tmp{i}", [P, D], F32) for i in range(2)]
        pw = [s.psum(f"pw{i}", [P, D]) for i in range(4)]
        pa = [s.psum(f"pa{i}", [P, D]) for i in range(4)]

        @s.block.sync
        def _(sp):
            sp.dma_start(wn[:], w_neigh_dram.rearrange("(c p) n -> p c n", p=P)).then_inc(s.w_in, 16)
            sp.wait_ge(s.w_in, 16)
            sp.dma_start(ws[:], w_self_dram.rearrange("(c p) n -> p c n", p=P)).then_inc(s.w_in, 16)
            sp.dma_start(bias[:], bias_dram.partition_broadcast(P)).then_inc(s.bias_in, 16)
            sp.wait_ge(s.w_in, 32)
            sp.wait_ge(s.bias_in, 16)

        @s.block.tensor
        def _(pe):
            pe.wait_ge(s.w_in, 16)
            for t in range(NT):
                if t >= 4:
                    pe.wait_ge(s.lo_ready, t - 3)
                for c in range(DC):
                    last = pe.matmul(pw[t % 4][:], g.ht[:, c, t * P:(t + 1) * P], wn[:, c, :],
                                     start=c == 0, stop=c == DC - 1)
                last.then_inc(s.y_ready, 1)
            pe.wait_ge(s.w_in, 32)
            for t in range(NT):
                k = (t + NT) % 4
                if t < 4:
                    pe.wait_ge(s.lo_ready, NT + t - 3)
                else:
                    pe.wait_ge(s.tile_read, t - 3)
                for c in range(DC):
                    pe.matmul(pw[k][:], g.ht[:, c, t * P:(t + 1) * P], ws[:, c, :], start=c == 0, stop=c == DC - 1)
                if t == 0:
                    pe.wait_ge(s.lo_ready, NT)
                for j in range(NT):
                    for part in (hi, lo):
                        last = pe.matmul(pa[k][:], g.by_src[:, j, t * P:(t + 1) * P], part[:, j, :],
                                         start=j == 0 and part is hi, stop=j == NT - 1 and part is lo)
                last.then_inc(s.tile_ready, 1)

        @s.block.scalar
        def _(act):
            for t in range(NT):
                act.wait_ge(s.y_ready, t + 1)
                act.activation(hi[:, t, :], pw[t % 4][:], ACT.Copy).then_inc(s.hi_ready, 1)

        @s.block.vector
        def _(dve):
            for t in range(NT):
                dve.wait_ge(s.hi_ready, t + 1)
                dve.tensor_tensor(lo[:, t, :], pw[t % 4][:], hi[:, t, :], ALU.subtract).then_inc(s.lo_ready, 1)
            dve.wait_ge(s.bias_in, 16)
            chain = Chain(dve, s.chain)
            for t in range(NT):
                k = (t + NT) % 4
                dve.wait_ge(s.tile_ready, t + 1)
                chain(dve.tensor_tensor(tmp[0][:], pw[k][:], bias[:], ALU.add))
                r = tmp[1][:] if add_to_x else g.rows[:, t, :]
                chain(dve.scalar_tensor_tensor(r, pa[k][:], g.rdeg_dst[:, t:t + 1], tmp[0][:], ALU.mult, ALU.add))
                dve.sem_inc(s.tile_read, 1)
                if add_to_x:
                    chain(dve.scalar_tensor_tensor(g.x[:, t, :], r, 0.0, g.x[:, t, :], ALU.max, ALU.add))
                elif relu:
                    chain(dve.tensor_scalar(r, r, 0.0, None, ALU.max))


def add_normed(nc, g, a):
    with stage(nc, "ln_out", "params_in", "stats", "chain", "var_ready", "root_ready") as s:
        gamma = s.sbuf("gamma", [P, D], F32)
        beta = s.sbuf("beta", [P, D], F32)
        stats = s.sbuf("stats", [P, NT, 6], F32)
        mv = s.sbuf("mv", [P, NT, 2], F32)
        var = s.sbuf("var", [P, NT], F32)
        root = s.sbuf("root", [P, NT], F32)
        rstd = s.sbuf("rstd", [P, NT], F32)

        @s.block.sync
        def _(sp):
            sp.dma_start(gamma[:], a.l2_gamma.partition_broadcast(P)).then_inc(s.params_in, 16)
            sp.dma_start(beta[:], a.l2_beta.partition_broadcast(P)).then_inc(s.params_in, 16)
            sp.wait_ge(s.params_in, 32)

        @s.block.scalar
        def _(act):
            act.wait_ge(s.var_ready, 1)
            act.activation(root[:], var[:], ACT.Sqrt).then_inc(s.root_ready, 1)

        @s.block.vector
        def _(dve):
            for t in range(NT):
                dve.bn_stats(stats[:, t, :], g.rows[:, t, :]).then_inc(s.stats, 1)
            dve.wait_ge(s.stats, NT)
            for t in range(NT):
                dve.bn_aggr(mv[:, t, :], stats[:, t, :]).then_inc(s.stats, 1)
            dve.wait_ge(s.stats, 2 * NT)
            chain = Chain(dve, s.chain)
            chain(dve.tensor_scalar(var[:], mv[:, :, 1], LN_EPS, None, ALU.add))
            dve.sem_inc(s.var_ready, 1)
            dve.wait_ge(s.root_ready, 1)
            newton_root(dve, chain, rstd[:], var[:], root[:])
            chain(dve.reciprocal(rstd[:], root[:]))
            dve.wait_ge(s.params_in, 32)
            for t in range(NT):
                r = g.rows[:, t, :]
                chain(dve.tensor_scalar(r, r, mv[:, t, 0:1], rstd[:, t:t + 1], ALU.subtract, ALU.mult))
                chain(dve.tensor_tensor(r, r, gamma[:], ALU.mult))
                chain(dve.tensor_tensor(r, r, beta[:], ALU.add))
                chain(dve.tensor_tensor(g.x[:, t, :], g.x[:, t, :], r, ALU.add))


def turn_rows(nc, g):
    with stage(nc, "turn", "tile_ready", "tile_kept") as s:
        pt = [s.psum(f"pt{i}", [P, DC, P]) for i in range(4)]

        @s.block.tensor
        def _(pe):
            for t in range(NT):
                if t >= 4:
                    pe.wait_ge(s.tile_kept, t - 3)
                for c in range(DC):
                    last = pe.transpose(pt[t % 4][:, c, :], g.rows[:, t, c * P:(c + 1) * P], g.ident[:])
                last.then_inc(s.tile_ready, 1)

        @s.block.scalar
        def _(act):
            for t in range(NT):
                act.wait_ge(s.tile_ready, t + 1)
                act.activation(g.ht[:, :, t * P:(t + 1) * P], pt[t % 4][:], ACT.Copy).then_inc(s.tile_kept, 1)


def linear_experts(nc, g, name, w_dram):
    B = 2 * NT
    with stage(nc, name, "w_in0", "w_in1", "y_ready", "y_added") as s:
        w = [s.sbuf(f"w{h}", [P, DC, D], F32) for h in range(2)]
        py = [s.psum(f"py{i}", [P, D]) for i in range(4)]
        w_in = [s.w_in0, s.w_in1]

        @s.block.sync
        def _(sp):
            with sp.Fori(0, E // 2) as i:
                for h in range(2):
                    sp.wait_ge(s.y_ready, i * B + (h + 1) * NT)
                    sp.dma_start(w[h][:], w_dram[bass.ds(i * 2 + h, 1)].rearrange("a (c p) n -> p (a c) n", p=P))\
                      .then_inc(w_in[h], 16)

        @s.block.tensor
        def _(pe):
            pe.sem_inc(s.y_ready, 2 * NT)
            with pe.Fori(0, E // 2) as i:
                for h in range(2):
                    pe.wait_ge(w_in[h], i * 16 + 16)
                    for t in range(NT):
                        v = h * NT + t
                        pe.wait_ge(s.y_added, i * B + v + 1)
                        for c in range(DC):
                            last = pe.matmul(py[v % 4][:], g.ht[:, c, t * P:(t + 1) * P], w[h][:, c, :],
                                             start=c == 0, stop=c == DC - 1)
                        last.then_inc(s.y_ready, 1)

        @s.block.vector
        def _(dve):
            dve.sem_inc(s.y_added, 4)
            with dve.Fori(0, E // 2) as i:
                for h in range(2):
                    for t in range(NT):
                        v = h * NT + t
                        dve.wait_ge(s.y_ready, i * B + v + 1 + 2 * NT)
                        dve.scalar_tensor_tensor(g.x[:, t, :], py[v % 4][:], g.gates[:, t, bass.ds(i * 2 + h, 1)],
                                                 g.x[:, t, :], ALU.mult, ALU.add).then_inc(s.y_added, 1)


def build(nc, a, out, until=None):
    ctx = ExitStack()
    with ctx:
        g = Kept()
        g.keep = lambda n, shape, dt: ctx.enter_context(nc.sbuf_tensor(n, shape, dt))
        g.x = g.keep("x", [P, NT, D], F32)
        g.ht = g.keep("ht", [P, DC, NP], F32)
        g.gates = g.keep("gates", [P, NT, E], F32)

        def steps():
            constants(nc, g)
            graph(nc, g, a)
            degrees(nc, g)
            yield "graph"
            layernorm(nc, g, "l0g")
            cheb(nc, g, a)
            yield "l0g"
            layernorm(nc, g, "l0f")
            route(nc, g, "l0f", a.l0_gate, "top2", capacity=-(-5 * N // (4 * E)))
            experts(nc, g, "l0f", 256, ACT.Gelu, a.l0_w1, a.l0_b1, a.l0_w2)
            expert_bias(nc, g, "l0f", a.l0_b2)
            yield "l0f"
            layernorm(nc, g, "l1g")
            with nc.sbuf_tensor("attn_out", [P, DC, NP], F32) as g.attn:
                attention(nc, g, a)
                batchnorm(nc, g, a)
            yield "l1g"
            layernorm(nc, g, "l1f")
            choose(nc, g, "l1f", a.l1_wr, min(512, N))
            experts(nc, g, "l1f", 256, ACT.Gelu, a.l1_w1, a.l1_b1, a.l1_w2)
            expert_bias(nc, g, "l1f", a.l1_b2)
            yield "l1f"
            layernorm(nc, g, "l2g")
            with nc.sbuf_tensor("rows", [P, NT, D], F32) as g.rows:
                sage(nc, g, "l2g", a.l2_w_self, a.l2_w_neigh, a.l2_bias, relu=False, add_to_x=False)
                add_normed(nc, g, a)
            yield "l2g"
            layernorm(nc, g, "l2f")
            route(nc, g, "l2f", a.l2_wr, "top1", bias_dram=a.l2_br)
            experts(nc, g, "l2f", 512, ACT.Relu, a.l2_w1, a.l2_b1, a.l2_w2)
            expert_bias(nc, g, "l2f", a.l2_b2)
            yield "l2f"
            layernorm(nc, g, "l3g")
            with nc.sbuf_tensor("rows3", [P, NT, D], F32) as g.rows:
                sage(nc, g, "l3g1", a.l3_w_self1, a.l3_w_neigh1, a.l3_b1, relu=True, add_to_x=False)
                turn_rows(nc, g)
                sage(nc, g, "l3g2", a.l3_w_self2, a.l3_w_neigh2, a.l3_b2, relu=True, add_to_x=True)
            yield "l3g"
            layernorm(nc, g, "l3f")
            route(nc, g, "l3f", a.l3_gate, "threshold", bias_dram=a.l3_gate_bias)
            expert_bias(nc, g, "l3f", a.l3_b)
            linear_experts(nc, g, "l3f", a.l3_w)
            yield "l3f"

        for name in steps():
            if name == until:
                break
        with stage(nc, "store", "stored") as s:
            @s.block.sync
            def _(sp):
                for t in range(NT):
                    n = min(P, N - t * P)
                    sp.dma_start(out[t * P:t * P + n, :], g.x[0:n, t, :]).then_inc(s.stored, 16)
                sp.wait_ge(s.stored, 16 * NT)


def laid_out(inputs):
    i = {k: np.asarray(v) for k, v in inputs.items()}

    def edges(v):
        z = np.full(ET * P, -1, np.int32)
        z[:NEDGE] = v
        return z.reshape(ET, P).T

    def by_chunk(w):
        return w.reshape(DC, P, -1).transpose(1, 0, 2)

    def bias_columns(b):
        return b.reshape(E, -1, P).transpose(0, 2, 1)

    x = np.zeros((NP, D), np.float32)
    x[:N] = i["x"]
    o = dict(
        x=x.reshape(NT, P, D).transpose(1, 0, 2), src=edges(i["src"]), dst=edges(i["dst"]),
        l0_w=i["L0_gnn_weight"], l0_bias=i["L0_gnn_bias"],
        l0_gate=by_chunk(i["L0_ffn_gate_w"].T), l0_w1=i["L0_ffn_w1"], l0_b1=bias_columns(i["L0_ffn_b1"]),
        l0_w2=i["L0_ffn_w2"], l0_b2=i["L0_ffn_b2"],
        wq=i["L1_gnn_Wq"], wk=i["L1_gnn_Wk"], wv=i["L1_gnn_Wv"],
        bn_gamma=i["L1_gnn_bn_gamma"].reshape(DC, P).T, bn_beta=i["L1_gnn_bn_beta"].reshape(DC, P).T,
        l1_wr=by_chunk(i["L1_ffn_Wr"]), l1_w1=i["L1_ffn_W1"], l1_b1=bias_columns(i["L1_ffn_b1"]),
        l1_w2=i["L1_ffn_W2"], l1_b2=i["L1_ffn_b2"],
        l2_w_self=i["L2_gnn_W_self"].T, l2_w_neigh=i["L2_gnn_W_neigh"].T, l2_bias=i["L2_gnn_bias"],
        l2_gamma=i["L2_gnn_gamma"], l2_beta=i["L2_gnn_beta"],
        l2_wr=by_chunk(i["L2_ffn_Wr"]), l2_br=i["L2_ffn_br"], l2_w1=i["L2_ffn_W1"],
        l2_b1=bias_columns(i["L2_ffn_b1"]), l2_w2=i["L2_ffn_W2"], l2_b2=i["L2_ffn_b2"],
        l3_w_self1=i["L3_gnn_W_self1"], l3_w_neigh1=i["L3_gnn_W_neigh1"], l3_b1=i["L3_gnn_b1"],
        l3_w_self2=i["L3_gnn_W_self2"], l3_w_neigh2=i["L3_gnn_W_neigh2"], l3_b2=i["L3_gnn_b2"],
        l3_gate=by_chunk(np.concatenate([i["L3_ffn_W_gate"], i["L3_ffn_W_thr"]], axis=1)),
        l3_gate_bias=np.concatenate([i["L3_ffn_b_gate"], i["L3_ffn_b_thr"]]),
        l3_w=i["L3_ffn_W_exp"], l3_b=i["L3_ffn_b_exp"],
    )
    return {f"{k}_in": np.ascontiguousarray(v) for k, v in o.items()}


def kernel(**inputs):
    import concourse.bacc as bacc
    from concourse.bass_utils import run_bass_kernel_spmd

    arrays = laid_out(inputs)
    nc = bacc.Bacc("TRN2", target_bir_lowering=False, num_devices=1)
    a = namedtuple("Inputs", [k[:-3] for k in arrays])(*(
        nc.dram_tensor(k, v.shape, mybir.dt.from_np(v.dtype), kind="ExternalInput").ap()
        for k, v in arrays.items()))
    out = nc.dram_tensor("out", (N, D), F32, kind="ExternalOutput").ap()
    build(nc, a, out)
    r = run_bass_kernel_spmd(nc, [arrays], core_ids=[0])
    return r.results[0]["out"]
```
